# Optimizing a Trainium2 kernel written in Bass

```python
import numpy as np
import jax
import jax.numpy as jnp

def _softmax(x, axis=-1):
    return jax.nn.softmax(x, axis=axis)

def _gelu(x):
    return jax.nn.gelu(x, approximate=True)

def _silu(x):
    return jax.nn.silu(x)

def _sigmoid(x):
    return jax.nn.sigmoid(x)

def _layernorm(x, axis=-1, eps=1e-05):
    m = jnp.mean(x, axis=axis, keepdims=True)
    v = jnp.var(x, axis=axis, keepdims=True)
    return (x - m) / jnp.sqrt(v + eps)

def _scatter_add(tgt, idx, src, axis=0):
    return tgt.at[idx].add(src)

def _segment_sum(src, seg, n):
    return jax.ops.segment_sum(src, seg, n)
kernel_name = 'mk_flamingo_gated_d1_seqx_r4_757078'

def setup_inputs(seed: int=0):
    np.random.seed(seed)
    _w = jnp.asarray

    def _rec_inputs():
        import jax
        import jax.numpy as jnp
        _rk = jax.random.key(seed)
        x = 7.22e-05 + 1 * jax.random.normal(jax.random.fold_in(_rk, 1), (8, 256, 256), jnp.float32)
        _lenS = 256 - jax.random.randint(jax.random.fold_in(_rk, 7), (8,), 0, max(1, 256 // 4) + 1, jnp.int32)
        _lenS2 = 120 - jax.random.randint(jax.random.fold_in(_rk, 8), (8,), 0, max(1, 120 // 4) + 1, jnp.int32)
        _ctx_1024P = jax.random.normal(jax.random.fold_in(_rk, 11), (8, 16, 256), jnp.float32)
        _ctx_1024c = jax.random.dirichlet(jax.random.fold_in(_rk, 511), 0.3 * jnp.ones((16,), jnp.float32), (8, 120))
        _ctx_1024t = jnp.einsum('bsk,bkd->bsd', _ctx_1024c, _ctx_1024P)
        _ctx_1024t = _ctx_1024t * jax.lax.rsqrt(jnp.mean(jnp.square(_ctx_1024t)) + 1e-12) * 0.953939
        ctx_1024 = 4.13588e-05 + 0.999923 * (_ctx_1024t + 0.3 * jax.random.normal(jax.random.fold_in(_rk, 611), (8, 120, 256), jnp.float32))
        _g = jax.random.normal(jax.random.fold_in(_rk, 9001), (2, 1), jnp.float32)
        _g = jnp.sign(_g) * jnp.maximum(jnp.abs(_g), 1.0) + (_g == 0) * 1.0
        g_xattn = _g[0]
        g_ffn = _g[1]
        return (x, ctx_1024, g_xattn, g_ffn)
    x, ctx_1024, g_xattn, g_ffn = _rec_inputs()

    def _L0_xattn_setup():
        import jax, jax.numpy as jnp
        import numpy as np
        HEADS = 16
        DIM_HEAD = 64
        DIM = 256
        CTX_DIM = 256
        INNER = HEADS * DIM_HEAD
        key = jax.random.key(seed)
        ks = jax.random.split(key, 6)
        b, n, m = (4, 512, 512)
        x = jax.random.normal(ks[0], (b, n, DIM), dtype=jnp.float32)
        context = jax.random.normal(ks[1], (b, m, CTX_DIM), dtype=jnp.float32)
        s = 0.02
        w_q = jax.random.normal(ks[2], (DIM, INNER), dtype=jnp.float32) * s
        w_kv = jax.random.normal(ks[3], (CTX_DIM, 2 * INNER), dtype=jnp.float32) * s
        w_out = jax.random.normal(ks[4], (INNER, DIM), dtype=jnp.float32) * s
        b_out = jnp.zeros((DIM,), dtype=jnp.float32)
        return {'x': x, 'context': context, 'w_q': w_q, 'w_kv': w_kv, 'w_out': w_out, 'b_out': b_out}
    _L0_xattn_all = _L0_xattn_setup()
    _L0_xattn_in = {k: v for k, v in _L0_xattn_all.items() if k in ('w_q', 'w_kv', 'w_out', 'b_out')}
    del _L0_xattn_all

    def _L0_ffn_setup():
        import jax, jax.numpy as jnp
        import numpy as np
        B, T, D = (2, 512, 256)
        E, DFF, TOPK = (8, 1024, 2)
        TEMPERATURE = 1.0
        key = jax.random.key(seed)
        k_x, k_w1, k_w2, k_r = jax.random.split(key, 4)
        x = jax.random.normal(k_x, (B, T, D), dtype=jnp.float32)
        W1 = jax.random.normal(k_w1, (E, DFF, D), dtype=jnp.float32) * 0.02
        W2 = jax.random.normal(k_w2, (E, D, DFF), dtype=jnp.float32) * 0.02
        Wr = jax.random.normal(k_r, (E, D), dtype=jnp.float32) * 0.02
        return {'x': x, 'W1': W1, 'W2': W2, 'Wr': Wr}
    _L0_ffn_all = _L0_ffn_setup()
    _L0_ffn_in = {k: v for k, v in _L0_ffn_all.items() if k in ('W1', 'W2', 'Wr')}
    del _L0_ffn_all
    return {'x': x, 'ctx_1024': ctx_1024, 'g_xattn': g_xattn, 'g_ffn': g_ffn, 'L0_xattn_w_q': _L0_xattn_in['w_q'], 'L0_xattn_w_kv': _L0_xattn_in['w_kv'], 'L0_xattn_w_out': _L0_xattn_in['w_out'], 'L0_xattn_b_out': _L0_xattn_in['b_out'], 'L0_ffn_W1': _L0_ffn_in['W1'], 'L0_ffn_W2': _L0_ffn_in['W2'], 'L0_ffn_Wr': _L0_ffn_in['Wr']}

def reference(x, ctx_1024, g_xattn, g_ffn, L0_xattn_w_q, L0_xattn_w_kv, L0_xattn_w_out, L0_xattn_b_out, L0_ffn_W1, L0_ffn_W2, L0_ffn_Wr):
    import jax
    import jax.numpy as jnp

    def _L0_xattn_ref(x, context, w_q, w_kv, w_out, b_out):
        import jax, jax.numpy as jnp
        import numpy as np
        HEADS = 16
        DIM_HEAD = 64
        DIM = 256
        CTX_DIM = 256
        INNER = HEADS * DIM_HEAD
        b, n, _ = x.shape
        m = context.shape[1]
        scale = DIM_HEAD ** (-0.5)
        q = (x @ w_q).reshape(b, n, HEADS, DIM_HEAD)
        kv = (context @ w_kv).reshape(b, m, 2, HEADS, DIM_HEAD)
        k, v = (kv[:, :, 0], kv[:, :, 1])
        attn = jnp.einsum('bnhd,bmhd->bhnm', q, k) * scale
        attn = jax.nn.softmax(attn, axis=-1)
        out = jnp.einsum('bhnm,bmhd->bnhd', attn, v).reshape(b, n, INNER)
        return out @ w_out + b_out

    def _L0_ffn_ref(x, W1, W2, Wr):
        import jax, jax.numpy as jnp
        import numpy as np
        B, T, D = (2, 512, 256)
        E, DFF, TOPK = (8, 1024, 2)
        TEMPERATURE = 1.0
        logits = jnp.einsum('btd,ed->bte', x, Wr)
        probs = jax.nn.softmax(logits / TEMPERATURE, axis=-1)
        topk_vals, topk_idx = jax.lax.top_k(probs, TOPK)
        router_weights = topk_vals / topk_vals.sum(-1, keepdims=True)
        one_hot = jax.nn.one_hot(topk_idx, E, dtype=x.dtype)
        gate = jnp.einsum('btk,btke->bte', router_weights, one_hot)
        h = jax.nn.silu(jnp.einsum('btd,efd->btef', x, W1))
        y = jnp.einsum('btef,edf->bted', h, W2)
        out = jnp.einsum('bte,bted->btd', gate, y)
        return out
    x = x + jnp.tanh(g_xattn[0]) * _L0_xattn_ref(_layernorm(x, axis=-1), ctx_1024, L0_xattn_w_q, L0_xattn_w_kv, L0_xattn_w_out, L0_xattn_b_out)
    x = x + jnp.tanh(g_ffn[0]) * _L0_ffn_ref(_layernorm(x, axis=-1), L0_ffn_W1, L0_ffn_W2, L0_ffn_Wr)
    return x

_drawn_inputs = setup_inputs


def setup_inputs(seed=0):
    import zlib

    import numpy as np

    out = dict(_drawn_inputs(seed))
    spreads = {'L0_xattn_b_out': (0.0, 0.1)}
    factors = {'L0_xattn_w_q': 8.0}
    for name, (base, spread) in spreads.items():
        noise = np.random.default_rng([zlib.crc32(name.encode()), seed]).standard_normal(out[name].shape)
        drawn = base * np.exp(spread * noise) if base else spread * noise
        out[name] = jnp.asarray(drawn.astype(out[name].dtype))
    for name, factor in factors.items():
        out[name] = (out[name] * factor).astype(out[name].dtype)
    return out
```

```python
from contextlib import ExitStack

import numpy as np

import concourse.bass as bass
from concourse import mybir

ALU = mybir.AluOpType
ACT = mybir.ActivationFunctionType
AX = mybir.AxisListType
F32 = mybir.dt.float32
F16 = mybir.dt.float16
I32 = mybir.dt.int32
U32 = mybir.dt.uint32
RMAX = bass.bass_isa.ReduceOp.max

P = 128
B, N, D = 8, 256, 256
M = 120
HEADS, DH = 16, 64
INNER = HEADS * DH
E, DFF = 8, 1024
T = B * N
KC = D // P
NT = N // P
TT = T // P
PAIRS = HEADS // 2
GH = 4
GROUPS = NT * HEADS // GH
IC = INNER // P
FC = DFF // P
TOPK = 2
TILES = TOPK * T // P + E - 1
BLOCKS = T // P
XG = 4
EPS = 1e-5
W2_EARLY, W2_LATE = (0, 1, 2, 3), (4, 6, 7, 5)

UP_W = 2.0 ** 14
UP_X = 2.0 ** 10
DOWN_Q = 2.0 ** -18
DOWN_KV = 2.0 ** -23
UP_H = 2.0 ** 6
LN_UP_P = float(np.log(4096.0))
EXPONENT = 0x7F800000
RSQRT_MAGIC = float(0x5F3759DF)

JOBS = [
    (0, "Ka", "n"),
    (1, "Kb", "n"), (1, "XT", "n"), (1, "Va", "n"),
    (2, "X2T0", "p"), (2, "OT1a", "p"), (2, "OT1b", "p"),
    (3, "LG0", "p"), (3, "Vb", "n"), (3, "PJ1", "p"), (3, "Q0", "n"),
    (4, "RK0", "p"), (4, "Q1", "n"),
    (5, "Q2", "n"), (5, "X2T1", "p"),
    (6, "OT0a", "c"), (6, "OT0b", "c"), (6, "LG1", "p"),
    (7, "Q3", "n"), (7, "RK1", "p"), (7, "PJ0", "c"),
]
PROLOGUE_JOBS = [(0, n, "n") for n in ("XT", "Ka", "Kb", "Va", "Vb", "Q0", "Q1", "Q2", "Q3")]
EPILOGUE_JOBS = [(8, "X2T0", "p"), (9, "LG0", "p"), (9, "OT1a", "p"), (9, "OT1b", "p"), (10, "RK0", "p"),
                 (10, "PJ1", "p"), (11, "X2T1", "p"), (12, "LG1", "p"), (13, "RK1", "p")]
JOB_BANKS = 3
HAS_HIGH = ("XT", "K", "V", "Q", "OT")


class Jobs:

    def __init__(self, jobs, k0, h0):
        self.at, self.steps, self.k0 = {}, {}, k0
        h = 0
        for i, (step, name, _) in enumerate(jobs):
            high = name.startswith(HAS_HIGH)
            job = (name, k0 + i, i % JOB_BANKS, h0 + h if high else None)
            self.at[name] = job
            self.steps.setdefault(step, []).append(job)
            h += high
        self.k_end, self.h_end = k0 + len(jobs), h0 + h


def batch_jobs(b, prev, nxt):
    jobs = [j for j in JOBS if (j[2] != "p" or prev) and (j[2] != "n" or nxt)]
    if not prev:
        return Jobs(jobs, len(PROLOGUE_JOBS), len(PROLOGUE_JOBS))
    high = sum(j[1].startswith(HAS_HIGH) for j in JOBS)
    first = len(PROLOGUE_JOBS) + sum(j[2] != "p" for j in JOBS)
    first_high = len(PROLOGUE_JOBS) + sum(j[2] != "p" and j[1].startswith(HAS_HIGH) for j in JOBS)
    return Jobs(jobs, (b - 1) * len(JOBS) + first, (b - 1) * high + first_high)


def epilogue_jobs():
    last = batch_jobs(B - 1, True, False)
    return Jobs(EPILOGUE_JOBS, last.k_end, last.h_end)


def run_batches(eng, body):
    body(0, 0, False, True)
    with eng.Fori(0, (B - 2) // 2) as i:
        body(i * 2 + 1, 1, True, True)
        body(i * 2 + 2, 0, True, True)
    body(B - 1, (B - 1) % 2, True, False)


def run_tiles(eng, step):
    step(0, 0, 1, 0, True, False)
    step(1, 1, 2, 0, False, False)
    with eng.Fori(0, (TILES - 3) // XG) as i:
        for j in range(XG):
            step(i * XG + 2 + j, j % 2, (3 + j) % XG, i + (3 + j) // XG, False, False)
    step(TILES - 1, (TILES - 1) % 2, None, None, False, True)


class Chain:

    def __init__(self, eng, sem):
        self.eng, self.sem, self.base, self.n = eng, sem, 0, 0

    def link(self, ins, constant=None):
        self.n += 1
        ins.then_inc(self.sem, 1)
        count = self.base + self.n
        if constant is not None and not isinstance(count, int):
            count = self.eng.to_reg(count)
            self.eng.wait_ge(constant, 1)
        self.eng.wait_ge(self.sem, count)


def build(nc, x, ctxT, wq, wkv, wo, bo, gx, gf, w1, w2, wr, out, xn2_dram, table):
    ctx = ExitStack()
    with ctx:
        def sem(name):
            return ctx.enter_context(nc.semaphore(name))

        def sb(name, shape, dt, scope=ctx):
            return scope.enter_context(nc.sbuf_tensor(name, shape, dt))

        w1s = sb("w1s", [P, E, 2, KC, DFF], F16)
        stage = [sb(f"stage{i}", [P, 2048], F32) for i in range(2)]
        ident = sb("ident", [P, P], F32)
        upper = sb("upper", [P, P], F16)
        ones = sb("ones", [P, P], F16)
        iota8 = sb("iota8", [P, E], F32)
        token = sb("token", [P, TT], F32)
        seg = sb("seg", [P, E], F32)
        tg = sb("tg", [P, 2], F32)
        amax = sb("amax", [P, 4], F32)
        amax_all = sb("amax_all", [P, 4], F32)
        pw = sb("pw", [P, 4], F32)
        up = sb("up", [P, 4], F32)
        tmp = sb("tmp", [P, 8], F32)
        logit_scale = sb("logit_scale", [P, 1], F32)
        attn_scale = sb("attn_scale", [P, 1], F32)

        row_id = sb("row_id", [P, 1], F32)
        tile_id = sb("tile_id", [P, TILES + 1], F32)
        base = [sb(f"base{i}", [P, E], F32) for i in range(2)]
        amc = [sb(f"amc{i}", [P, 5], F32) for i in range(2)]
        amc_all = [sb(f"amc_all{i}", [P, 5], F32) for i in range(2)]
        pw1 = sb("pw1", [P, E], F32)
        pw2 = sb("pw2", [P, E], F32)
        upw = [sb(f"upw{i}", [P, 1], F32) for i in range(2)]
        amc2 = sb("amc2", [P, E, 5], F32)
        amc2_all = sb("amc2_all", [P, E, 5], F32)
        upw2 = sb("upw2", [P, E], F32)
        small8 = sb("small8", [P, 8, E], F32)
        small8i = sb("small8i", [P, 2, E], I32)
        blk = sb("blk", [P, 1], I32)
        expert_of = sb("expert_of", [P, TILES], I32)
        z_scale = sb("z_scale", [P, TILES], F32)
        h_scale = sb("h_scale", [P, TILES], F32)
        y_scale = sb("y_scale", [P, TILES], F32)
        row_of = sb("row_of", [P, TILES], I32)

        att = ctx.enter_context(ExitStack())
        wqs = sb("wqs", [P, 2, KC, INNER], F16, att)
        wkvs = sb("wkvs", [P, 2, KC, 2 * INNER], F16, att)
        ctxs = sb("ctxs", [P, 2, KC, B * M], F16, att)
        qT, kT, v = [None] * 2, [None] * 2, [None] * 2

        def heads(i):
            qT[i] = sb(f"qT{i}", [P, 2, PAIRS, N], F16, att)
            kT[i] = sb(f"kT{i}", [P, 2, PAIRS, 2 * M], F16, att)
            v[i] = sb(f"v{i}", [M, 2, HEADS, DH + 1], F16, att)

        heads(0)
        xin = sb("xin", [P, NT, D], F32, att)
        xn = sb("xn", [P, NT, D], F32, att)
        xnT = sb("xnT", [P, 2, KC, N], F16, att)
        taken = 4 * KC * (3 * INNER + B * M) + 4 * PAIRS * (N + 2 * M) + 4 * HEADS * (DH + 1) + 4 * NT * D + 4 * NT * D \
            + 4 * KC * N
        sb("gap", [P, E * 4 * DFF * KC - taken], mybir.dt.uint8, att)
        heads(1)
        wos = sb("wos", [P, 2, IC, D], F16, att)
        wrs = sb("wrs", [P, KC, E], F32, att)
        bout = sb("bout", [P, D], F32, att)
        xres = [sb(f"xres{i}", [P, D], F32, att) for i in range(2)]
        pr = [sb(f"pr{i}", [P, GH, M], F32, att) for i in range(2)]
        pT = [sb(f"pT{i}", [M, 2, GH, P], F16, att) for i in range(2)]
        o = [sb(f"o{i}", [P, INNER], F32, att) for i in range(2)]
        oT = sb("oT", [P, 2, IC, P], F16, att)
        x2 = [sb(f"x2_{i}", [P, D], F32, att) for i in range(2)]
        xn2 = [sb(f"xn2_{i}", [P, D], F32, att) for i in range(2)]
        xn2T = [sb(f"xn2T{i}", [P, KC, P], F32, att) for i in range(2)]
        stats = sb("stats", [P, TT, 6], F32, att)
        mv = sb("mv", [P, TT, 2], F32, att)
        ln_a = sb("ln_a", [P, 4, TT], F32, att)
        ln_scale = sb("ln_scale", [P, TT], F32, att)
        ln_shift = sb("ln_shift", [P, TT], F32, att)
        nmax = [sb(f"nmax{i}", [P, GH], F32, att) for i in range(2)]
        ebias = [sb(f"ebias{i}", [P, GH], F32, att) for i in range(2)]
        rsum = [sb(f"rsum{i}", [P, GH], F32, att) for i in range(2)]
        stats2 = [sb(f"stats2_{i}", [P, 6], F32, att) for i in range(2)]
        mv2 = [sb(f"mv2_{i}", [P, 2], F32, att) for i in range(2)]
        ln_b = [sb(f"ln_b{i}", [P, 6], F32, att) for i in range(2)]
        logits = [sb(f"logits{i}", [P, E], F32, att) for i in range(2)]
        top = [sb(f"top{i}", [P, 8], F32, att) for i in range(2)]
        top_at = [sb(f"top_at{i}", [P, 8], U32, att) for i in range(2)]
        top_f = [sb(f"top_f{i}", [P, TOPK], F32, att) for i in range(2)]
        chosen = [sb(f"chosen{i}", [P, TOPK, E], F32, att) for i in range(2)]
        mask = [sb(f"mask{i}", [P, E], F16, att) for i in range(2)]
        slot_e = [sb(f"slot_e{i}", [P, E], F32, att) for i in range(2)]
        slot_m = [sb(f"slot_m{i}", [P, TOPK, E], F32, att) for i in range(2)]
        slot_f = [sb(f"slot_f{i}", [P, TOPK], F32, att) for i in range(2)]
        slot = [sb(f"slot{i}", [P, TOPK], I32, att) for i in range(2)]
        ratio = [sb(f"ratio{i}", [P, 2], F32, att) for i in range(2)]
        entry = [sb(f"entry{i}", [P, TOPK, 2], F32, att) for i in range(2)]
        pad = sb("pad", [P, P, 2], F32, att)
        att.close()

        w2s = sb("w2s", [P, E, 2, FC, D], F16)
        land = [sb(f"land{i}", [P, FC * D], F32) for i in range(2)]
        found = sb("found", [P, 2 * P], F32)
        by_expert = sb("by_expert", [P, TILES, E], F32)
        one_hot = sb("one_hot", [P, TILES, E], F32)
        expert_f = sb("expert_f", [P, TILES], F32)
        gate_y = sb("gate_y", [P, TILES], F32)
        xg = [sb(f"xg{i}", [P, D], F32) for i in range(XG)]
        xsT = [sb(f"xsT{i}", [P, 2, KC, P], F16) for i in range(2)]
        hf = [sb(f"hf{i}", [P, DFF], F32) for i in range(2)]
        hT = [sb(f"hT{i}", [P, 2, FC, P], F16) for i in range(2)]
        yt = [sb(f"yt{i}", [P, D], F32) for i in range(2)]

        raw = w1s[:].rearrange("p e s k f -> p (e s k f)").bitcast(F32)
        raw_kv = raw[:, 0:4096].rearrange("p (k n) -> p k n", k=KC)
        raw_q = raw[:, 4096:6144].rearrange("p (k n) -> p k n", k=KC)
        raw_o = raw[:, 6144:8192].rearrange("p (k n) -> p k n", k=IC)
        raw_ctx = raw[:, 8192:8192 + KC * B * M].rearrange("p (k n) -> p k n", k=KC)
        x_all = [s[:].rearrange("p (t d) -> p t d", d=D) for s in stage]

        def pb(name):
            return ctx.enter_context(nc.psum_tensor(name, [P, 512], F32))

        s_bank = [pb(f"s_bank{i}") for i in range(2)]
        t_bank = pb("t_bank")
        o_bank = [pb(f"o_bank{i}") for i in range(2)]
        j_bank = [pb(f"j_bank{i}") for i in range(JOB_BANKS)]
        z_bank, hT_bank = o_bank, [t_bank, j_bank[2]]

        const_done = sem("const_done")
        raw_in = [sem(f"raw_in{i}") for i in range(4)]
        small_in = sem("small_in")
        x_all_in = [sem(f"x_all_in{i}") for i in range(2)]
        xin_in = sem("xin_in")
        xres_in = [sem(f"xres_in{i}") for i in range(NT)]
        zero_done = sem("zero_done")
        amax_done = sem("amax_done")
        allmax_done = sem("allmax_done")
        scales_done = sem("scales_done")
        tanh_done = sem("tanh_done")
        w_high = sem("w_high")
        w_low = sem("w_low")
        dve_chain = sem("dve_chain")
        pool_chain = sem("pool_chain")
        xn_done = sem("xn_done")
        job_full = sem("job_full")
        job_high = sem("job_high")
        job_free = sem("job_free")
        scores_full = sem("scores_full")
        bias_done = sem("bias_done")
        exp_done = sem("exp_done")
        pT_full = sem("pT_full")
        pT_high = sem("pT_high")
        pT_low = sem("pT_low")
        av_full = sem("av_full")
        norm_done = sem("norm_done")
        xb_done = sem("xb_done")
        spare_zero = sem("spare_zero")
        xn2_out = [sem(f"xn2_out{i}") for i in range(NT)]
        ln2_start = sem("ln2_start")
        ln2_done = sem("ln2_done")
        xn2_done = sem("xn2_done")
        top_done = sem("top_done")
        mask_done = sem("mask_done")
        ratio_done = sem("ratio_done")
        route_done = sem("route_done")
        table_in = sem("table_in")
        scattered = sem("scattered")
        slots_free = sem("slots_free")
        stage_in = [sem(f"stage_in{i}") for i in range(2)]
        amc_done = sem("amc_done")
        amc_reduced = sem("amc_reduced")
        upw_done = sem("upw_done")
        stage_high = sem("stage_high")
        stage_low = sem("stage_low")
        w2_in = [sem(f"w2_in{e}") for e in range(E)]
        amc_summed = sem("amc_summed")
        blk_done = sem("blk_done")
        found_in = sem("found_in")
        found_T = sem("found_T")
        tables_done = sem("tables_done")
        rows_done = sem("rows_done")
        xg_in = [sem(f"xg_in{i}") for i in range(XG)]
        xs_full = sem("xs_full")
        xs_high = sem("xs_high")
        xs_low = sem("xs_low")
        z_full = sem("z_full")
        hT_full = sem("hT_full")
        silu_done = sem("silu_done")
        h_high = sem("h_high")
        h_low = sem("h_low")
        y_full = sem("y_full")
        y_done = sem("y_done")
        y_added = sem("y_added")
        x2_out = [sem(f"x2_out{i}") for i in range(NT)]

        x_v = x.rearrange("(t p) d -> p t d", p=P)
        x_b = x.rearrange("(b t p) d -> b p t d", t=NT, p=P)
        out_t = out.rearrange("(t p) d -> t p d", p=P)
        x_t = x.rearrange("(t p) d -> t p d", p=P)
        xn2_t = xn2_dram.rearrange("(t p) d -> t p d", p=P)
        table_b = table.rearrange("(b r) c -> b (r c)", r=P)
        w1_v = w1.rearrange("e p k f -> e p (k f)")
        w2_v = w2.rearrange("e p c d -> e p (c d)")

        def w1_part(e, part, c):
            return w1s[:, bass.ds(e, 1), part].rearrange("p e k f -> p (e k f)")[:, c:c + 512]

        def w2_part(e, part, c):
            return w2s[:, e, part].rearrange("p c d -> p (c d)")[:, c:c + 512]

        w2_raw = [w2s[:, 4 + e].rearrange("p s c d -> p (s c d)").bitcast(F32) for e in range(4)]
        w2_raw += [t[:] for t in (*stage, *land)]

        SPLITS = ((raw_ctx, ctxs, 0), (raw_kv, wkvs, 1), (raw_q, wqs, 2), (raw_o, wos, 3))

        block = ctx.enter_context(nc.Block())

        @block.sync
        def _(sp):
            for i in range(2):
                sp.dma_start(x_all[i], x_v[:, 8 * i:8 * i + 8, :]).then_inc(x_all_in[i], 16)
            sp.dma_start(raw_ctx, ctxT).then_inc(raw_in[0], 16)
            sp.dma_start(raw_kv, wkv).then_inc(raw_in[1], 16)
            sp.dma_start(raw_q, wq).then_inc(raw_in[2], 16)
            sp.dma_start(raw_o, wo).then_inc(raw_in[3], 16)
            sp.dma_start(xin[:], x_b[0]).then_inc(xin_in, 16)

            sp.wait_ge(spare_zero, 1)
            sp.dma_start(out[T:T + P, :], x2[1][:]).then_inc(x2_out[1], 16)
            for i in range(2):
                sp.dma_start(xn2_dram[T + 64 * i:T + 64 * i + 64, :], x2[1][64 * i:64 * i + 64, :]).then_inc(xn2_out[i], 16)
            sp.wait_ge(const_done, 9)
            sp.dma_start(table_b[0:P, :], pad[:].rearrange("p r c -> p (r c)")).then_inc(table_in, 16)
            sp.dma_start(table_b[P:P + 1, :], pad[0:1].rearrange("p r c -> p (r c)")).then_inc(table_in, 16)
            sp.wait_ge(xn_done, 1)
            sp.dma_start(stage[0][:], w1_v[0]).then_inc(stage_in[0], 16)

            def store(b, nt):
                sp.dma_start(out_t[bass.ds(b * 2 + nt, 1)].rearrange("a p d -> p (a d)"), x2[nt][:]).then_inc(x2_out[nt], 16)

            def store_norm(b, nt):
                sp.wait_ge(xn2_done, b * 2 + nt + 1)
                sp.dma_start(xn2_t[bass.ds(b * 2 + nt, 1)].rearrange("a p d -> p (a d)"), xn2[nt][:]).then_inc(xn2_out[nt], 16)

            def body(b, parity, prev, nxt):
                jobs = batch_jobs(b, prev, nxt)
                if nxt:
                    sp.wait_ge(xn_done, b + 1)
                    sp.dma_start(xin[:], x_b[bass.ds(b + 1, 1)].rearrange("a p t d -> p (a t) d")).then_inc(xin_in, 16)
                sp.dma_start(xres[0][:], x_t[bass.ds(b * 2, 1)].rearrange("a p d -> p (a d)")).then_inc(xres_in[0], 16)
                if prev:
                    store_norm(b - 1, 0)
                    sp.wait_ge(job_free, jobs.at["PJ1"][1] + 1)
                    store(b - 1, 1)
                if not nxt:
                    for e in range(4):
                        sp.dma_start(w2_raw[e], w2_v[e]).then_inc(w2_in[e], 16)
                sp.dma_start(xres[1][:], x_t[bass.ds(b * 2 + 1, 1)].rearrange("a p d -> p (a d)")).then_inc(xres_in[1], 16)
                if prev:
                    store_norm(b - 1, 1)
                    sp.wait_ge(stage_low, b * 4)
                if nxt:
                    sp.dma_start(stage[1 - parity][:], w1_v[bass.ds(b + 1, 1)].rearrange("a p n -> p (a n)")).then_inc(
                        stage_in[1 - parity], 16)
                else:
                    sp.dma_start(w2_raw[4], w2_v[4]).then_inc(w2_in[4], 16)
                sp.wait_ge(job_free, jobs.at["PJ0"][1] + 1)
                store(b, 0)

            run_batches(sp, body)
            store_norm(B - 1, 0)
            sp.wait_ge(job_free, epilogue_jobs().at["PJ1"][1] + 1)
            store(B - 1, 1)
            store_norm(B - 1, 1)
            sp.wait_ge(norm_done, B * GROUPS)
            for e in (6, 7):
                sp.dma_start(w2_raw[e], w2_v[e]).then_inc(w2_in[e], 16)
            sp.wait_ge(stage_low, 4 * E)
            sp.dma_start(w2_raw[5], w2_v[5]).then_inc(w2_in[5], 16)
            sp.wait_ge(x2_out[0], 16 * B)
            sp.wait_ge(x2_out[1], 16 * (B + 1))

        @block.gpsimd
        def _(pool):
            pool.memset(ident[:], 0.0).then_inc(pool_chain, 1)
            pool.memset(upper[:], 1.0).then_inc(pool_chain, 1)
            pool.memset(ones[:], 1.0).then_inc(const_done, 1)
            pool.iota(iota8[:], [[1, E]], base=0, channel_multiplier=0,
                      allow_small_or_imprecise_dtypes=True).then_inc(const_done, 1)
            pool.iota(token[:], [[P, TT]], base=0, channel_multiplier=1,
                      allow_small_or_imprecise_dtypes=True).then_inc(const_done, 1)
            pool.iota(seg[:], [[T, E]], base=0, channel_multiplier=0,
                      allow_small_or_imprecise_dtypes=True).then_inc(const_done, 1)
            pool.iota(row_id[:], [[0, 1]], base=0, channel_multiplier=1,
                      allow_small_or_imprecise_dtypes=True).then_inc(const_done, 1)
            pool.iota(tile_id[:], [[1, TILES + 1]], base=0, channel_multiplier=0,
                      allow_small_or_imprecise_dtypes=True).then_inc(const_done, 1)
            pool.memset(pad[:], 0.0).then_inc(pool_chain, 1)
            pool.wait_ge(pool_chain, 3)
            pool.iota(pad[:, :, 0], [[1, P]], base=T, channel_multiplier=0,
                      allow_small_or_imprecise_dtypes=True).then_inc(const_done, 1)
            pool.affine_select(out=ident[:], in_=ident[:], compare_op=ALU.not_equal, fill=1.0, base=0,
                               pattern=[[-1, P]], channel_multiplier=1).then_inc(const_done, 1)
            pool.affine_select(out=upper[:], in_=upper[:], compare_op=ALU.is_gt, fill=0.0, base=0,
                               pattern=[[1, P]], channel_multiplier=-1).then_inc(const_done, 1)
            pool.wait_ge(amax_done, 4)
            pool.partition_all_reduce(amax_all[:], amax[:], P, RMAX).then_inc(allmax_done, 1)

            pool.sem_inc(slots_free, 1)

            chain = Chain(pool, pool_chain)
            chain.base = 3

            def residual(m):
                pool.wait_ge(xres_in[m % 2], 16 * (m // 2 + 1))
                if m == 0:
                    pool.wait_ge(tanh_done, 2)
                pool.tensor_tensor(xres[m % 2][:], xres[m % 2][:], bout[:], ALU.add).then_inc(xb_done, 1)

            def norm_scale(m):
                c, y, a, sc, sh = (ln_b[m % 2][:, k:k + 1] for k in (0, 1, 2, 3, 4))
                pool.wait_ge(ln2_start, m + 1)
                for _ in range(3):
                    chain.link(pool.tensor_scalar(a, y, y, c, ALU.mult, ALU.mult))
                    chain.link(pool.tensor_scalar(a, a, -0.5, 1.5, ALU.mult, ALU.add))
                    chain.link(pool.tensor_tensor(y, y, a, ALU.mult))
                chain.link(pool.tensor_scalar(sc, y, UP_X, None, ALU.mult))
                chain.link(pool.tensor_scalar(a, mv2[m % 2][:, 0:1], -1.0, None, ALU.mult))
                pool.tensor_tensor(sh, a, sc, ALU.mult).then_inc(ln2_done, 1)

            def scatter(m):
                pool.wait_ge(route_done, m + 1)
                if m == 0:
                    pool.wait_ge(table_in, 32)
                for k in range(TOPK):
                    if m or k:
                        pool.wait_ge(scattered, 16 * (m * TOPK + k))
                    if k == 0:
                        pool.sem_inc(slots_free, 1)
                    pool.indirect_dma_start(out=table[:], out_offset=bass.IndirectOffsetOnAxis(slot[m % 2][:, k:k + 1], 0),
                                            in_=entry[m % 2][:, k, :], in_offset=None).then_inc(scattered, 16)

            def reduce_stage(q):
                pool.wait_ge(amc_done, q + 1)
                pool.partition_all_reduce(amc_all[q % 2][:], amc[q % 2][:], P, RMAX).then_inc(amc_reduced, 1)

            def split_low(q, chunks):
                for k in chunks:
                    pool.wait_ge(stage_high, 4 * q + k + 1)
                    c = 512 * k
                    chunk = stage[q % 2][:, c:c + 512]
                    chain.link(pool.tensor_scalar(chunk, chunk, upw[q % 2][:], None, ALU.mult))
                    pool.tensor_tensor(w1_part(q, 1, c), chunk, w1_part(q, 0, c), ALU.subtract).then_inc(stage_low, 1)

            def reduce_w2(late):
                g = slice(4 * late, 4 * late + 4)
                pool.wait_ge(amc_done, E + 1 + late)
                pool.wait_ge(amc_summed, 1 + late)
                pool.partition_all_reduce(amc2_all[:, g].rearrange("p e k -> p (e k)"), amc2[:, g].rearrange("p e k -> p (e k)"),
                                          P, RMAX).then_inc(amc_reduced, 1)

            for b in range(B + 1):
                if b < B:
                    residual(2 * b)
                if 0 < b < B:
                    split_low(b - 1, (0, 1))
                if b:
                    norm_scale(2 * b - 1)
                if b < B:
                    reduce_stage(b)
                else:
                    reduce_w2(False)
                if 0 < b < B:
                    split_low(b - 1, (2,))
                if b:
                    scatter(2 * b - 2)
                if 0 < b < B:
                    split_low(b - 1, (3,))
                if b < B:
                    residual(2 * b + 1)
                    norm_scale(2 * b)
                if b:
                    scatter(2 * b - 1)

            pool.wait_ge(blk_done, 1)
            pool.wait_ge(scattered, 16 * TT * TOPK)
            pool.indirect_dma_start(out=found[0:TILES, :], out_offset=None, in_=table_b,
                                    in_offset=bass.IndirectOffsetOnAxis(blk[0:TILES, :], 0)).then_inc(found_in, 16)
            reduce_w2(True)

            def gather(t):
                if t >= XG:
                    pool.wait_ge(xs_full, t - XG + 1)
                pool.indirect_dma_start(out=xg[t % XG][:], out_offset=None, in_=xn2_dram[:],
                                        in_offset=bass.IndirectOffsetOnAxis(row_of[:, t:t + 1], 0)).then_inc(xg_in[t % XG], 16)

            pool.wait_ge(rows_done, 1)
            for i in range(NT):
                pool.wait_ge(xn2_out[i], 16 * (B + 1))
                pool.wait_ge(x2_out[i], 16 * (B + i))
            for t in range(XG):
                gather(t)
            for t in range(TILES):
                if t and t + XG - 1 < TILES:
                    gather(t + XG - 1)
                pool.wait_ge(y_done, t + 1)
                if t:
                    pool.wait_ge(y_added, 16 * t)
                pool.indirect_dma_start(out=out[:], out_offset=bass.IndirectOffsetOnAxis(row_of[:, t:t + 1], 0),
                                        in_=yt[t % 2][:], in_offset=None, compute_op=ALU.add).then_inc(y_added, 16)
            pool.wait_ge(y_added, 16 * TILES)

        @block.scalar
        def _(act):
            act.dma_start(tg[:, 0:1], gx.unsqueeze(0).to_broadcast((P, 1))).then_inc(small_in, 16)
            act.dma_start(tg[:, 1:2], gf.unsqueeze(0).to_broadcast((P, 1))).then_inc(small_in, 16)
            act.dma_start(bout[:], bo.unsqueeze(0).to_broadcast((P, D))).then_inc(small_in, 16)
            act.dma_start(wrs[:], wr).then_inc(small_in, 16)
            act.wait_ge(small_in, 64)
            nc.scalar.activation(tg[:], tg[:], ACT.Tanh).then_inc(tanh_done, 1)
            act.wait_ge(scales_done, 1)
            for src, dst, i in SPLITS:
                for k in range(src.shape[1]):
                    nc.scalar.activation(dst[:, 0, k, :], src[:, k, :], ACT.Copy,
                                         scale=up[:, i:i + 1]).then_inc(w_high, 1)

            def job(j, par):
                name, k, bank, h = j
                src = j_bank[bank]
                if h is None:
                    return
                act.wait_ge(job_full, k + 1)
                if name == "XT":
                    nc.scalar.activation(xnT[:, 0].rearrange("p k n -> p (k n)"), src[:], ACT.Copy).then_inc(job_high, 1)
                elif name[0] == "K":
                    c = 4 * (name == "Kb")
                    for a in range(2):
                        ins = nc.scalar.activation(kT[par][64 * a:64 * a + 64, 0, c:c + 4, a * M:a * M + M],
                                                   src[64 * a:64 * a + 64, 0:4 * M].rearrange("p (c m) -> p c m", m=M),
                                                   ACT.Copy, scale=DOWN_KV)
                    ins.then_inc(job_high, 1)
                elif name[0] == "V":
                    c = 8 * (name == "Vb")
                    nc.scalar.activation(v[par][:, 0, c:c + 8, 0:DH], src[0:M, :].rearrange("p (h d) -> p h d", d=DH),
                                         ACT.Copy, scale=DOWN_KV).then_inc(job_high, 1)
                elif name[0] == "Q":
                    c = 2 * int(name[1])
                    nc.scalar.activation(qT[par][:, 0, c:c + 2, :], src[:].rearrange("p (c n) -> p c n", c=2),
                                         ACT.Copy, scale=DOWN_Q).then_inc(job_high, 1)
                else:
                    c = 4 * (name[3] == "b")
                    nc.scalar.activation(oT[:, 0, c:c + 4, :], src[:].rearrange("p (c n) -> p c n", c=4),
                                         ACT.Copy).then_inc(job_high, 1)

            def pT_split(g, s):
                act.wait_ge(pT_full, g + 1)
                nc.scalar.activation(pT[s % 2][:, 0], t_bank[0:M, :].rearrange("p (h n) -> p h n", h=GH),
                                     ACT.Copy).then_inc(pT_high, 1)

            def exps(g, s, prev):
                act.wait_ge(bias_done, g + 1)
                if prev or s >= 2:
                    act.wait_ge(pT_full, g - 1)
                for h in range(GH):
                    ins = nc.scalar.activation(pr[s % 2][:, h, :], s_bank[s % 2][:, h * M:(h + 1) * M], ACT.Exp,
                                               bias=ebias[s % 2][:, h:h + 1], scale=logit_scale[:])
                ins.then_inc(exp_done, 1)

            for j in Jobs(PROLOGUE_JOBS, 0, 0).steps[0]:
                job(j, 0)

            def gate_ratio(b, nt):
                act.wait_ge(top_done, b * 2 + nt + 1)
                nc.scalar.activation(ratio[nt][:, 0:1], top[nt][:, 0:1], ACT.Exp, bias=top[nt][:, 1:2],
                                     scale=-1.0).then_inc(ratio_done, 1)

            def split_high(q, par, k):
                if k == 0:
                    act.wait_ge(upw_done, q + 1)
                c = 512 * k
                nc.scalar.activation(w1_part(q, 0, c), stage[par][:, c:c + 512], ACT.Copy,
                                     scale=upw[par][:]).then_inc(stage_high, 1)

            def w2_sums(experts, done, junk):
                for n, e in enumerate(experts):
                    act.wait_ge(w2_in[e], 16)
                    for k in (2, 3):
                        ins = nc.scalar.activation(junk(2 * n + k - 2), w2_raw[e][:, 512 * k:512 * k + 512], ACT.Abs,
                                                   accum_out=amc2[:, e, k:k + 1])
                if done:
                    ins.then_inc(amc_summed, 1)

            def w2_high(e):
                act.wait_ge(upw_done, E + 1 + e // 4)
                if e >= 4:
                    act.wait_ge(stage_low, (E + e - 3) * 4)
                for k in range(4):
                    c = 512 * k
                    nc.scalar.activation(w2_part(e, 0, c), w2_raw[e][:, c:c + 512], ACT.Copy,
                                         scale=upw2[:, e:e + 1]).then_inc(stage_high, 1)

            def body(b, parity, prev, nxt):
                jobs = batch_jobs(b, prev, nxt)
                for s in range(GROUPS):
                    js = jobs.steps.get(s, [])
                    exps(b * 8 + s, s, prev)
                    for j in js[:1]:
                        job(j, 1 - parity)
                    if prev or s >= 1:
                        pT_split(b * 8 + s - 1, s - 1)
                    for j in js[1:]:
                        job(j, 1 - parity)
                    if prev and s in (3, 7):
                        gate_ratio(b - 1, s // 4)
                    if prev and s < 4:
                        split_high(b - 1, 1 - parity, s)

            run_batches(act, body)
            jobs = epilogue_jobs()
            pT_split(8 * B - 1, 7)
            for s in range(8, 14):
                for j in jobs.steps.get(s, []):
                    job(j, 0)
                if s in (10, 13):
                    gate_ratio(B - 1, int(s == 13))
                if s < 12:
                    split_high(B - 1, 1, s - 8)
                if s == 11:
                    w2_sums(W2_EARLY, True, lambda n: w2_part(n // 2, 0, 512 * (n % 2)))
            spare = [t[:].rearrange("p a c n -> p (a c n)")[:, 512 * k:512 * k + 512] for t in hT for k in range(4)]
            for e in W2_EARLY:
                w2_high(e)
                if e == 1:
                    w2_sums(W2_LATE[:3], False, lambda n: spare[n])
            w2_sums(W2_LATE[3:], True, lambda n: spare[6 + n])
            for e in range(4, E):
                w2_high(e)

            def x_high(t, par, first):
                act.wait_ge(xs_full, t + 1)
                if not first:
                    act.wait_ge(z_full, t * 2 - 2)
                nc.scalar.activation(xsT[par][:, 0].rearrange("p k n -> p (k n)"), s_bank[par][:, 0:D],
                                     ACT.Copy).then_inc(xs_high, 1)

            def later(sem, t, a):
                count = t * 2 + a + 1 if isinstance(t, int) else act.to_reg(t * 2 + a + 1)
                act.wait_ge(tables_done, 1)
                act.wait_ge(sem, count)

            def silu(t, par):
                for a in range(2):
                    later(z_full, t, a)
                    nc.scalar.activation(hf[par][:, 512 * a:512 * a + 512], z_bank[a][:], ACT.Silu,
                                         scale=z_scale[:, bass.ds(t, 1)]).then_inc(silu_done, 1)

            def h_split(t, par):
                for a in range(2):
                    later(hT_full, t, a)
                    nc.scalar.activation(hT[par][:, 0, 4 * a:4 * a + 4, :], hT_bank[a][:].rearrange("p (c n) -> p c n", c=4),
                                         ACT.Copy, scale=h_scale[:, bass.ds(t, 1)]).then_inc(h_high, 1)

            act.wait_ge(tables_done, 1)
            x_high(0, 0, True)

            def step(t, par, buf, before, first, last):
                if not last:
                    x_high(t + 1, 1 - par, first)
                silu(t, par)
                h_split(t, par)

            run_tiles(act, step)

        @block.vector
        def _(dve):
            chain = Chain(dve, dve_chain)

            for i in range(2):
                for h in range(2):
                    nc.vector.memset(kT[i][64:128, h, :, 0:M], 0.0)
                    nc.vector.memset(kT[i][0:64, h, :, M:2 * M], 0.0)
                    nc.vector.memset(v[i][:, h, :, DH:DH + 1], 1.0 - h).then_inc(zero_done, 1)
            nc.vector.memset(x2[1][:], 0.0).then_inc(spare_zero, 1)
            for i in range(2):
                nc.vector.memset(amc[i][:, 4:5], 1e-30)
            nc.vector.memset(amc2[:, :, 4:5], 1e-30)
            dve.wait_ge(const_done, 9)
            chain.link(nc.vector.tensor_copy(base[0][:], seg[:]))
            for t in range(TT):
                if t % 8 == 0:
                    dve.wait_ge(x_all_in[t // 8], 16)
                ins = nc.vector.bn_stats(stats[:, t, :], x_all[t // 8][:, t % 8, :])
            chain.link(ins)
            for t in range(TT):
                ins = nc.vector.bn_aggr(mv[:, t, :], stats[:, t, :])
            chain.link(ins)

            def rsqrt(var, y, a, c):
                chain.link(nc.vector.tensor_scalar(c, var, EPS, None, ALU.add))
                chain.link(nc.vector.tensor_scalar(a.bitcast(U32), c.bitcast(U32), 1, None, ALU.logical_shift_right))
                chain.link(nc.vector.tensor_scalar(y.bitcast(I32), a.bitcast(I32), -1.0, RSQRT_MAGIC, ALU.mult, ALU.add))
                for _ in range(3):
                    chain.link(nc.vector.tensor_tensor(a, y, y, ALU.mult))
                    chain.link(nc.vector.tensor_tensor(a, a, c, ALU.mult))
                    chain.link(nc.vector.tensor_scalar(a, a, -0.5, 1.5, ALU.mult, ALU.add))
                    chain.link(nc.vector.tensor_tensor(y, y, a, ALU.mult))

            rsqrt(mv[:, :, 1], ln_a[:, 0, :], ln_a[:, 1, :], ln_a[:, 2, :])
            chain.link(nc.vector.tensor_scalar(ln_scale[:], ln_a[:, 0, :], UP_X, None, ALU.mult))
            chain.link(nc.vector.scalar_tensor_tensor(out=ln_shift[:], in0=mv[:, :, 0], scalar=-1.0, in1=ln_scale[:],
                                                      op0=ALU.mult, op1=ALU.mult))

            def norm_x(b):
                dve.wait_ge(xin_in, (b + 1) * 16)
                for t in range(NT):
                    ins = nc.vector.tensor_scalar(xn[:, t, :], xin[:, t, :], ln_scale[:, bass.ds(b * 2 + t, 1)],
                                                  ln_shift[:, bass.ds(b * 2 + t, 1)], ALU.mult, ALU.add)
                ins.then_inc(xn_done, 1)

            norm_x(0)
            for i, (src, _, _) in enumerate(SPLITS):
                dve.wait_ge(raw_in[i], 16)
                nc.vector.tensor_reduce(amax[:, i:i + 1], src.rearrange("p k n -> p (k n)"), AX.X, ALU.max,
                                        apply_absolute_value=True).then_inc(amax_done, 1)
            dve.wait_ge(allmax_done, 1)
            chain.link(nc.vector.tensor_scalar(pw[:], amax_all[:], 1e-30, None, ALU.max))
            chain.link(nc.vector.tensor_scalar(pw[:].bitcast(U32), pw[:].bitcast(U32), EXPONENT, None, ALU.bitwise_and))
            chain.link(nc.vector.reciprocal(up[:], pw[:]))
            chain.link(nc.vector.tensor_scalar(up[:], up[:], UP_W, None, ALU.mult))
            chain.link(nc.vector.tensor_tensor(tmp[:, 0:1], pw[:, 0:1], pw[:, 1:2], ALU.mult))
            chain.link(nc.vector.scalar_tensor_tensor(out=logit_scale[:], in0=tmp[:, 0:1], scalar=2.0 ** -14,
                                                      in1=pw[:, 2:3], op0=ALU.mult, op1=ALU.mult))
            dve.wait_ge(tanh_done, 1)
            chain.link(nc.vector.scalar_tensor_tensor(out=tmp[:, 1:2], in0=tmp[:, 0:1], scalar=2.0 ** -19,
                                                      in1=pw[:, 3:4], op0=ALU.mult, op1=ALU.mult))
            chain.link(nc.vector.tensor_tensor(attn_scale[:], tmp[:, 1:2], tg[:, 0:1], ALU.mult))
            nc.vector.tensor_scalar(bout[:], bout[:], tg[:, 0:1], None, ALU.mult).then_inc(tanh_done, 1)
            nc.vector.tensor_scalar(tmp[:, 2:3], up[:, 0:1], 1.0, None, ALU.mult).then_inc(scales_done, 1)
            n = 0
            for src, dst, i in SPLITS:
                for k in range(src.shape[1]):
                    n += 1
                    dve.wait_ge(w_high, n)
                    nc.vector.scalar_tensor_tensor(out=dst[:, 1, k, :], in0=src[:, k, :], scalar=up[:, i:i + 1],
                                                   in1=dst[:, 0, k, :], op0=ALU.mult,
                                                   op1=ALU.subtract).then_inc(w_low, 1)

            def low(dst, src, high, scale, inc):
                if scale == 1.0:
                    ins = nc.vector.tensor_tensor(dst, src, high, ALU.subtract)
                else:
                    ins = nc.vector.scalar_tensor_tensor(out=dst, in0=src, scalar=scale, in1=high,
                                                         op0=ALU.mult, op1=ALU.subtract)
                if inc is not None:
                    ins.then_inc(inc, 1)

            def job(j, par, b, prev_b, first=False):
                name, k, bank, h = j
                src = j_bank[bank]
                if h is not None:
                    dve.wait_ge(job_high, h + 1)
                else:
                    dve.wait_ge(job_full, k + 1)
                if name == "XT":
                    low(xnT[:, 1].rearrange("p k n -> p (k n)"), src[:], xnT[:, 0].rearrange("p k n -> p (k n)"), 1.0, job_free)
                elif name[0] == "K":
                    c = 4 * (name == "Kb")
                    for a in range(2):
                        r, cols = slice(64 * a, 64 * a + 64), slice(a * M, a * M + M)
                        low(kT[par][r, 1, c:c + 4, cols], src[r, 0:4 * M].rearrange("p (c m) -> p c m", m=M),
                            kT[par][r, 0, c:c + 4, cols], DOWN_KV, job_free if a else None)
                elif name[0] == "V":
                    c = 8 * (name == "Vb")
                    low(v[par][:, 1, c:c + 8, 0:DH], src[0:M, :].rearrange("p (h d) -> p h d", d=DH),
                        v[par][:, 0, c:c + 8, 0:DH], DOWN_KV, job_free)
                elif name[0] == "Q":
                    c = 2 * int(name[1])
                    low(qT[par][:, 1, c:c + 2, :], src[:].rearrange("p (c n) -> p c n", c=2),
                        qT[par][:, 0, c:c + 2, :], DOWN_Q, job_free)
                elif name[:2] == "OT":
                    c = 4 * (name[3] == "b")
                    low(oT[:, 1, c:c + 4, :], src[:].rearrange("p (c n) -> p c n", c=4), oT[:, 0, c:c + 4, :], 1.0, job_free)
                elif name[:2] == "PJ":
                    nt = int(name[2])
                    mb = (prev_b if nt else b) * 2 + nt
                    dve.wait_ge(xb_done, mb + 1)
                    if nt:
                        dve.wait_ge(x2_out[1], prev_b * 16 + 16)
                    elif not first:
                        dve.wait_ge(x2_out[0], b * 16)
                    nc.vector.scalar_tensor_tensor(out=x2[nt][:], in0=src[:, 0:D], scalar=attn_scale[:], in1=xres[nt][:],
                                                   op0=ALU.mult, op1=ALU.add).then_inc(job_free, 1)
                    dve.wait_ge(job_free, k + 1)
                    norm2_start(nt)
                elif name[:3] == "X2T":
                    nc.vector.tensor_copy(xn2T[int(name[3])][:].rearrange("p k n -> p (k n)"), src[:, 0:D]).then_inc(job_free, 1)
                elif name[:2] == "LG":
                    nt = int(name[2])
                    nc.vector.tensor_scalar(logits[nt][:], src[:, 0:E], 1.0 / UP_X, None, ALU.mult).then_inc(job_free, 1)
                    dve.wait_ge(const_done, 1)
                    dve.wait_ge(job_free, k + 1)
                    choose(nt)
                else:
                    nt = int(name[2])
                    chain.link(nc.vector.tensor_tensor(slot_e[nt][:], src[:, 0:E], base[nt][:], ALU.add))
                    nc.vector.tensor_tensor(base[1 - nt][:], src[:, E:2 * E], base[nt][:], ALU.add).then_inc(job_free, 1)

            def norm2_start(nt):
                c, y, a = (ln_b[nt][:, k:k + 1] for k in range(3))
                chain.link(nc.vector.bn_stats(stats2[nt][:], x2[nt][:]), const_done)
                chain.link(nc.vector.bn_aggr(mv2[nt][:], stats2[nt][:]))
                chain.link(nc.vector.tensor_scalar(c, mv2[nt][:, 1:2], EPS, None, ALU.add))
                chain.link(nc.vector.tensor_scalar(a.bitcast(U32), c.bitcast(U32), 1, None, ALU.logical_shift_right))
                nc.vector.tensor_scalar(y.bitcast(I32), a.bitcast(I32), -1.0, RSQRT_MAGIC, ALU.mult,
                                        ALU.add).then_inc(ln2_start, 1)

            def norm2(b, nt):
                dve.wait_ge(ln2_done, b * 2 + nt + 1)
                dve.wait_ge(xn2_out[nt], b * 16 + 16)
                nc.vector.tensor_scalar(xn2[nt][:], x2[nt][:], ln_b[nt][:, 3:4], ln_b[nt][:, 4:5], ALU.mult,
                                        ALU.add).then_inc(xn2_done, 1)

            def choose(nt):
                chain.link(nc.vector.max(top[nt][:], logits[nt][:]), const_done)
                chain.link(nc.vector.max_index(top_at[nt][:], top[nt][:], logits[nt][:]))
                chain.link(nc.vector.tensor_copy(top_f[nt][:], top_at[nt][:, 0:TOPK]))
                nc.vector.tensor_scalar(chosen[nt][:, 0, :], iota8[:], top_f[nt][:, 0:1], None, ALU.is_equal).then_inc(top_done, 1)
                chain.link(nc.vector.tensor_scalar(chosen[nt][:, 1, :], iota8[:], top_f[nt][:, 1:2], None, ALU.is_equal))
                nc.vector.tensor_tensor(mask[nt][:], chosen[nt][:, 0, :], chosen[nt][:, 1, :], ALU.add).then_inc(mask_done, 1)

            def route(b, nt):
                m = b * 2 + nt
                chain.link(nc.vector.tensor_tensor(slot_m[nt][:], chosen[nt][:],
                                                   slot_e[nt][:].unsqueeze(1).to_broadcast([P, TOPK, E]), ALU.mult))
                chain.link(nc.vector.tensor_reduce(slot_f[nt][:], slot_m[nt][:], AX.X, ALU.add))
                dve.wait_ge(slots_free, m + 1)
                nc.vector.tensor_copy(slot[nt][:], slot_f[nt][:])
                for c in range(TOPK):
                    nc.vector.tensor_copy(entry[nt][:, c, 0:1], token[:, bass.ds(m, 1)])
                dve.wait_ge(ratio_done, m + 1)
                chain.link(nc.vector.tensor_scalar(ratio[nt][:, 1:2], ratio[nt][:, 0:1], 1.0, None, ALU.add))
                chain.link(nc.vector.reciprocal(entry[nt][:, 0, 1:2], ratio[nt][:, 1:2]))
                nc.vector.tensor_tensor(entry[nt][:, 1, 1:2], entry[nt][:, 0, 1:2], ratio[nt][:, 0:1],
                                        ALU.mult).then_inc(route_done, 1)

            def stage_max(q, par, k):
                if k == 0:
                    dve.wait_ge(stage_in[par], q // 2 * 16 + 16 if isinstance(q, int) else stage_count(q, par))
                ins = nc.vector.tensor_reduce(amc[par][:, k:k + 1], stage[par][:, 512 * k:512 * k + 512], AX.X, ALU.max,
                                              apply_absolute_value=True)
                if k == 3:
                    ins.then_inc(amc_done, 1)

            def stage_count(q, par):
                return (q - par) * 8 + 16

            def stage_scale(n, power, bounds, up):
                dve.wait_ge(amc_reduced, n)
                chain.link(nc.vector.tensor_reduce(power, bounds, AX.X, ALU.max))
                chain.link(nc.vector.tensor_scalar(power.bitcast(U32), power.bitcast(U32), EXPONENT, None, ALU.bitwise_and),
                           const_done)
                chain.link(nc.vector.reciprocal(up, power))
                nc.vector.tensor_scalar(up, up, UP_W, None, ALU.mult).then_inc(upw_done, 1)

            def w2_max(experts, done):
                for e in experts:
                    dve.wait_ge(w2_in[e], 16)
                    for k in range(2):
                        ins = nc.vector.tensor_reduce(amc2[:, e, k:k + 1], w2_raw[e][:, 512 * k:512 * k + 512], AX.X, ALU.max,
                                                      apply_absolute_value=True)
                if done:
                    ins.then_inc(amc_done, 1)

            def w2_scale(late):
                g = slice(4 * late, 4 * late + 4)
                stage_scale(E + 1 + late, pw2[:, g], amc2_all[:, g], upw2[:, g])

            def w1_low(k):
                c = 512 * k
                dve.wait_ge(stage_high, 4 * (E - 1) + k + 1)
                nc.vector.scalar_tensor_tensor(out=w1_part(E - 1, 1, c), in0=stage[1][:, c:c + 512], scalar=upw[1][:],
                                               in1=w1_part(E - 1, 0, c), op0=ALU.mult, op1=ALU.subtract).then_inc(stage_low, 1)

            def split_low(e):
                for k in range(4):
                    dve.wait_ge(stage_high, 4 * (E + e) + k + 1)
                    c = 512 * k
                    nc.vector.scalar_tensor_tensor(out=w2_part(e, 1, c), in0=w2_raw[e][:, c:c + 512], scalar=upw2[:, e:e + 1],
                                                   in1=w2_part(e, 0, c), op0=ALU.mult, op1=ALU.subtract).then_inc(stage_low, 1)

            def group_max(g, s, prev):
                dve.wait_ge(scores_full, g + 1)
                if prev or s >= 2:
                    dve.wait_ge(exp_done, g - 1)
                chain.link(nc.vector.tensor_reduce(nmax[s % 2][:], s_bank[s % 2][:, 0:GH * M].rearrange("p (h m) -> p h m", h=GH),
                                                   AX.X, ALU.max, negate=True))
                nc.vector.tensor_scalar(ebias[s % 2][:], nmax[s % 2][:], logit_scale[:], LN_UP_P, ALU.mult,
                                        ALU.add).then_inc(bias_done, 1)

            def pT_split(g, s):
                dve.wait_ge(pT_high, g + 1)
                low(pT[s % 2][:, 1], t_bank[0:M, :].rearrange("p (h n) -> p h n", h=GH), pT[s % 2][:, 0], 1.0, pT_low)

            def norm_o(g, s):
                bank = o_bank[s % 2][:, 0:GH * (DH + 1)].rearrange("p (h d) -> p h d", h=GH)
                dve.wait_ge(av_full, g + 1)
                chain.link(nc.vector.reciprocal(rsum[s % 2][:], bank[:, :, DH]))
                c = (s % 4) * GH * DH
                nc.vector.tensor_tensor(o[s % 8 // 4][:, c:c + GH * DH].rearrange("p (h d) -> p h d", h=GH), bank[:, :, 0:DH],
                                        rsum[s % 2][:].unsqueeze(2).to_broadcast([P, GH, DH]), ALU.mult).then_inc(norm_done, 1)

            for j in Jobs(PROLOGUE_JOBS, 0, 0).steps[0]:
                job(j, 0, 0, 0)

            LINKS = 45
            group_max(0, 0, False)

            def body(b, parity, prev, nxt):
                jobs = batch_jobs(b, prev, nxt)
                if prev:
                    chain.base, chain.n = (b - 1) * LINKS + after_first, 0
                for s in range(GROUPS):
                    js = jobs.steps.get(s, [])
                    if s == 0 and nxt:
                        norm_x(b + 1)
                    for j in js[:1]:
                        job(j, 1 - parity, b, b - 1, not prev)
                    if prev or s >= 1:
                        pT_split(b * 8 + s - 1, s - 1)
                    if s < 7 or nxt:
                        group_max(b * 8 + s + 1, (s + 1) % 8, prev or s >= 1)
                    for j in js[1:2]:
                        job(j, 1 - parity, b, b - 1, not prev)
                    if prev or s >= 2:
                        norm_o(b * 8 + s - 2, s - 2)
                    for j in js[2:]:
                        job(j, 1 - parity, b, b - 1, not prev)
                    if prev and s in (0, 4):
                        norm2(b - 1, s // 4)
                    if prev and s in (5, 7):
                        route(b - 1, int(s == 7))
                    if s < 4:
                        stage_max(b, parity, s)
                    if s == 7:
                        stage_scale(b + 1, pw1[:, bass.ds(b, 1)], amc_all[parity][:], upw[parity][:])
                assert not prev or not nxt or chain.n == LINKS, chain.n

            body(0, 0, False, True)
            after_first = chain.base + chain.n
            with dve.Fori(0, (B - 2) // 2) as i:
                body(i * 2 + 1, 1, True, True)
                body(i * 2 + 2, 0, True, True)
            body(B - 1, (B - 1) % 2, True, False)
            jobs = epilogue_jobs()
            norm2(B - 1, 0)
            pT_split(8 * B - 1, 7)
            norm_o(8 * B - 2, 6)
            for s in range(8, 14):
                if s == 9:
                    norm_o(8 * B - 1, 7)
                if s == 11:
                    norm2(B - 1, 1)
                for j in jobs.steps.get(s, []):
                    job(j, 0, B, B - 1)
                if s == 9:
                    dve.wait_ge(stage_low, 4 * (E - 1))
                    w1_low(0)
                if s == 10:
                    w1_low(1)
                if s == 11:
                    w1_low(2)
                    w2_max(W2_EARLY, True)
                    w1_low(3)
                if s == 13:
                    w2_scale(False)
                if s in (11, 13):
                    route(B - 1, int(s == 13))

            count, tiles, upto, frm, cmp_p, e_p, f_p, y8 = (small8[:, k, :] for k in range(8))
            h8 = tmp[:, 0:E]
            chain.link(nc.vector.tensor_tensor(count, base[0][:], seg[:], ALU.subtract))
            chain.link(nc.vector.tensor_scalar(small8i[:, 0, :], count, float(P - 1), None, ALU.add))
            chain.link(nc.vector.tensor_scalar(small8i[:, 1, :], small8i[:, 0, :], 7, None, ALU.arith_shift_right))
            chain.link(nc.vector.tensor_copy(tiles, small8i[:, 1, :]))
            chain.link(nc.vector.memset(count, 1.0))
            chain.link(nc.vector.tensor_tensor_scan(upto, count, tiles, 0.0, ALU.mult, ALU.add))
            chain.link(nc.vector.tensor_tensor(frm, upto, tiles, ALU.subtract))
            chain.link(nc.vector.tensor_scalar(cmp_p, upto, row_id[:], None, ALU.is_le))
            chain.link(nc.vector.tensor_reduce(e_p[:, 0:1], cmp_p, AX.X, ALU.add))
            chain.link(nc.vector.tensor_scalar(f_p, iota8[:], e_p[:, 0:1], None, ALU.is_equal))
            chain.link(nc.vector.tensor_tensor(cmp_p, f_p, frm, ALU.mult))
            chain.link(nc.vector.tensor_reduce(e_p[:, 1:2], cmp_p, AX.X, ALU.add))
            chain.link(nc.vector.tensor_tensor(e_p[:, 2:3], row_id[:], e_p[:, 1:2], ALU.subtract))
            chain.link(nc.vector.scalar_tensor_tensor(out=e_p[:, 3:4], in0=e_p[:, 0:1], scalar=float(BLOCKS), in1=e_p[:, 2:3],
                                                      op0=ALU.mult, op1=ALU.add))
            nc.vector.tensor_scalar(blk[:], e_p[:, 3:4], float(E * BLOCKS), None, ALU.min).then_inc(blk_done, 1)
            chain.link(nc.vector.tensor_tensor(by_expert[:], upto.unsqueeze(1).to_broadcast([P, TILES, E]),
                                               tile_id[:, 0:TILES].unsqueeze(2).to_broadcast([P, TILES, E]), ALU.is_le))
            chain.link(nc.vector.tensor_reduce(expert_f[:], by_expert[:], AX.X, ALU.add))
            chain.link(nc.vector.tensor_scalar(expert_f[:], expert_f[:], float(E - 1), None, ALU.min))
            nc.vector.tensor_copy(expert_of[:], expert_f[:])
            chain.link(nc.vector.tensor_tensor(one_hot[:], iota8[:].unsqueeze(1).to_broadcast([P, TILES, E]),
                                               expert_f[:].unsqueeze(2).to_broadcast([P, TILES, E]), ALU.is_equal))

            for e in W2_EARLY:
                split_low(e)
                if e == 1:
                    w2_max(W2_LATE[:3], False)
            w2_max(W2_LATE[3:], True)
            w2_scale(True)
            for e in range(4, E):
                split_low(e)

            chain.link(nc.vector.scalar_tensor_tensor(out=y8, in0=pw1[:], scalar=2.0 ** -20, in1=pw2[:], op0=ALU.mult,
                                                      op1=ALU.mult))
            chain.link(nc.vector.tensor_scalar(y8, y8, tg[:, 1:2], None, ALU.mult))
            chain.link(nc.vector.reciprocal(h8, pw1[:]))
            chain.link(nc.vector.tensor_scalar(h8, h8, UP_H, None, ALU.mult))
            chain.link(nc.vector.tensor_scalar(count, pw1[:], 1.0 / (UP_W * UP_X), None, ALU.mult))
            for vec, dst in ((count, z_scale), (h8, h_scale), (y8, y_scale)):
                chain.link(nc.vector.tensor_tensor(by_expert[:], one_hot[:], vec.unsqueeze(1).to_broadcast([P, TILES, E]),
                                                   ALU.mult))
                chain.link(nc.vector.tensor_reduce(dst[:], by_expert[:], AX.X, ALU.add))
            nc.vector.tensor_copy(tmp[:, 0:1], z_scale[:, 0:1]).then_inc(tables_done, 1)
            dve.wait_ge(found_T, 1)
            nc.vector.tensor_copy(row_of[:], j_bank[0][:, 0:TILES]).then_inc(rows_done, 1)
            chain.link(nc.vector.tensor_tensor(gate_y[:], j_bank[0][:, 64:64 + TILES], y_scale[:], ALU.mult))

            def x_low(t, par):
                dve.wait_ge(xs_high, t + 1)
                nc.vector.tensor_tensor(xsT[par][:, 1].rearrange("p k n -> p (k n)"), s_bank[par][:, 0:D],
                                        xsT[par][:, 0].rearrange("p k n -> p (k n)"), ALU.subtract).then_inc(xs_low, 1)

            def h_split(t, par):
                for a in range(2):
                    dve.wait_ge(h_high, t * 2 + a + 1)
                    nc.vector.scalar_tensor_tensor(out=hT[par][:, 1, 4 * a:4 * a + 4, :],
                                                   in0=hT_bank[a][:].rearrange("p (c n) -> p c n", c=4),
                                                   scalar=h_scale[:, bass.ds(t, 1)], in1=hT[par][:, 0, 4 * a:4 * a + 4, :],
                                                   op0=ALU.mult, op1=ALU.subtract).then_inc(h_low, 1)

            def y_gated(t, par, first):
                dve.wait_ge(y_full, t + 1)
                if not first:
                    dve.wait_ge(y_added, t * 16 - 16)
                nc.vector.tensor_scalar(yt[par][:], j_bank[par][:, 0:D], gate_y[:, bass.ds(t, 1)], None,
                                        ALU.mult).then_inc(y_done, 1)

            x_low(0, 0)

            def step(t, par, buf, before, first, last):
                if not last:
                    x_low(t + 1, 1 - par)
                if not first:
                    y_gated(t - 1, 1 - par, isinstance(t, int) and t < 3)
                h_split(t, par)

            run_tiles(dve, step)
            y_gated(TILES - 1, (TILES - 1) % 2, False)

        @block.tensor
        def _(pe):
            pe.wait_ge(const_done, 9)

            def three(out, lhs, rhs):
                n = len(lhs)
                for i in range(n):
                    for a, c in ((0, 0), (0, 1), (1, 0)):
                        ins = pe.matmul(out, lhs[i](a), rhs[i](c), start=(i == 0 and a + c == 0),
                                        stop=(i == n - 1 and a == 1))
                return ins

            def job(j, par, b, jobs):
                name, k, bank, h = j
                dst = j_bank[bank]
                if not (isinstance(k, int) and k < JOB_BANKS):
                    pe.wait_ge(job_free, k - JOB_BANKS + 1)
                if name == "XT":
                    pe.wait_ge(xn_done, b + 1)
                    for kc in range(KC):
                        for t in range(NT):
                            ins = pe.transpose(dst[:, (kc * NT + t) * P:(kc * NT + t + 1) * P],
                                               xn[:, t, kc * P:(kc + 1) * P], ident[:])
                elif name[0] == "K":
                    c = 4 * (name == "Kb")
                    for q in range(4):
                        ins = three(dst[:, q * M:(q + 1) * M],
                                    [lambda a, kc=kc, q=q: wkvs[:, a, kc, (c + q) * P:(c + q + 1) * P] for kc in range(KC)],
                                    [lambda a, kc=kc: ctxs[:, a, kc, bass.ds(b * M, M)] for kc in range(KC)])
                elif name[0] == "V":
                    c = INNER + 512 * (name == "Vb")
                    ins = three(dst[0:M, :],
                                [lambda a, kc=kc: ctxs[:, a, kc, bass.ds(b * M, M)] for kc in range(KC)],
                                [lambda a, kc=kc: wkvs[:, a, kc, c:c + 512] for kc in range(KC)])
                elif name[0] == "Q":
                    if name == "Q0":
                        pe.wait_ge(job_free, jobs.at["XT"][1] + 1)
                    c = 2 * int(name[1])
                    for q in range(2):
                        ins = three(dst[:, q * N:(q + 1) * N],
                                    [lambda a, kc=kc, q=q: wqs[:, a, kc, (c + q) * P:(c + q + 1) * P] for kc in range(KC)],
                                    [lambda a, kc=kc: xnT[:, a, kc, :] for kc in range(KC)])
                elif name[:2] == "OT":
                    nt, half = int(name[2]), name[3] == "b"
                    pe.wait_ge(norm_done, (b * 2 + nt) * 4 + 4)
                    for q in range(4):
                        c = (4 * half + q) * P
                        ins = pe.transpose(dst[:, q * P:(q + 1) * P], o[nt][:, c:c + P], ident[:])
                elif name[:2] == "PJ":
                    pe.wait_ge(job_free, jobs.at["OT" + name[2] + "b"][1] + 1)
                    ins = three(dst[:, 0:D], [lambda a, ic=ic: oT[:, a, ic, :] for ic in range(IC)],
                                [lambda a, ic=ic: wos[:, a, ic, :] for ic in range(IC)])
                elif name[:3] == "X2T":
                    nt = int(name[3])
                    pe.wait_ge(xn2_done, b * 2 + nt + 1)
                    for kc in range(KC):
                        ins = pe.transpose(dst[:, kc * P:(kc + 1) * P], xn2[nt][:, kc * P:(kc + 1) * P], ident[:])
                elif name[:2] == "LG":
                    nt = int(name[2])
                    pe.wait_ge(job_free, jobs.at["X2T" + name[2]][1] + 1)
                    for kc in range(KC):
                        ins = pe.matmul(dst[:, 0:E], xn2T[nt][:, kc, :], wrs[:, kc, :], start=(kc == 0), stop=(kc == KC - 1))
                else:
                    nt = int(name[2])
                    pe.wait_ge(mask_done, b * 2 + nt + 1)
                    pe.matmul(dst[:, 0:E], upper[:], mask[nt][:], start=True, stop=True)
                    ins = pe.matmul(dst[:, E:2 * E], ones[:], mask[nt][:], start=True, stop=True)
                ins.then_inc(job_full, 1)

            def scores(g, s, par, prev):
                if prev or s >= 2:
                    pe.wait_ge(exp_done, g - 1)
                for q in range(2):
                    pair, t = 2 * (s % 4) + q, s // 4
                    ins = three(s_bank[s % 2][:, q * 2 * M:(q + 1) * 2 * M],
                                [lambda a: qT[par][:, a, pair, t * P:(t + 1) * P]], [lambda a: kT[par][:, a, pair, :]])
                ins.then_inc(scores_full, 1)

            def transposes(g, s, first):
                pe.wait_ge(exp_done, g + 1)
                if not first:
                    pe.wait_ge(pT_low, g)
                for h in range(GH):
                    ins = pe.transpose(t_bank[0:M, h * P:(h + 1) * P], pr[s % 2][:, h, :], ident[:])
                ins.then_inc(pT_full, 1)

            def values(g, s, par, first):
                pe.wait_ge(pT_low, g + 1)
                if not first:
                    pe.wait_ge(norm_done, g - 1)
                for h in range(GH):
                    head = (s % 4) * GH + h
                    ins = three(o_bank[s % 2][:, h * (DH + 1):(h + 1) * (DH + 1)],
                                [lambda a: pT[s % 2][:, a, h, :]], [lambda a: v[par][:, a, head, :]])
                ins.then_inc(av_full, 1)

            pe.wait_ge(w_low, KC * 3 + IC)
            pe.wait_ge(zero_done, 4)
            pro = Jobs(PROLOGUE_JOBS, 0, 0)
            for j in pro.steps[0]:
                job(j, 0, 0, pro)

            pe.wait_ge(job_free, len(PROLOGUE_JOBS))
            scores(0, 0, 0, False)
            KIND = {name: kind for _, name, kind in JOBS}
            AFTER_Q3 = len(JOBS) - 1 - [name for _, name, _ in JOBS].index("Q3")

            def body(b, parity, prev, nxt):
                jobs = batch_jobs(b, prev, nxt)

                def run(js):
                    for j in js:
                        kind = KIND[j[0]]
                        job(j, 1 - parity, b + 1 if kind == "n" else b - 1 if kind == "p" else b, jobs)

                for s in range(GROUPS):
                    js = jobs.steps.get(s, [])
                    if s < 7:
                        if s == 0 and prev:
                            pe.wait_ge(job_free, jobs.k0 - AFTER_Q3)
                        scores(b * 8 + s + 1, s + 1, parity, prev or s >= 1)
                    elif nxt:
                        pe.wait_ge(job_free, jobs.at["Q0"][1] + 1)
                        scores(b * 8 + 8, 0, 1 - parity, True)
                    run(js[:1])
                    if prev or s >= 1:
                        transposes(b * 8 + s - 1, (s - 1) % 8, not prev and s < 2)
                    run(js[1:2])
                    if prev or s >= 2:
                        values(b * 8 + s - 2, (s - 2) % 8, parity if s >= 2 else 1 - parity, not prev and s < 4)
                    run(js[2:])

            run_batches(pe, body)
            jobs = epilogue_jobs()
            transposes(8 * B - 1, 7, False)
            values(8 * B - 2, 6, (B - 1) % 2, False)
            for s in range(8, 14):
                if s == 9:
                    values(8 * B - 1, 7, (B - 1) % 2, False)
                for j in jobs.steps.get(s, []):
                    job(j, 0, B - 1, jobs)

            pe.wait_ge(found_in, 16)
            pe.wait_ge(job_free, jobs.k_end)
            f = found[0:TILES, :].rearrange("t (r c) -> t r c", c=2)
            pe.transpose(j_bank[0][:, 0:TILES], f[:, :, 0], ident[0:TILES, 0:TILES])
            pe.transpose(j_bank[0][:, 64:64 + TILES], f[:, :, 1], ident[0:TILES, 0:TILES]).then_inc(found_T, 1)

            def tile_T(t, par, buf, before, first):
                pe.wait_ge(xg_in[buf], before * 16 + 16)
                if not first:
                    pe.wait_ge(xs_low, t - 1)
                for kc in range(KC):
                    ins = pe.transpose(s_bank[par][:, kc * P:(kc + 1) * P], xg[buf][:, kc * P:(kc + 1) * P], ident[:])
                ins.then_inc(xs_full, 1)

            def expert(t):
                return pe.value_load(expert_of[0:1, bass.ds(t, 1)], min_val=0, max_val=E - 1)

            def up_product(e, t, par, first):
                pe.wait_ge(xs_low, t + 1)
                if not first:
                    pe.wait_ge(silu_done, t * 2)
                for a in range(2):
                    three(z_bank[a][:], [lambda p, kc=kc: xsT[par][:, p, kc, :] for kc in range(KC)],
                          [lambda p, kc=kc: w1s[:, bass.ds(e, 1), p, kc, 512 * a:512 * a + 512].rearrange("p e f -> p (e f)")
                           for kc in range(KC)]).then_inc(z_full, 1)

            def hidden_T(t, par, first):
                if not first:
                    pe.wait_ge(h_low, t * 2)
                for a in range(2):
                    pe.wait_ge(silu_done, t * 2 + a + 1)
                    for c in range(4):
                        ins = pe.transpose(hT_bank[a][:, c * P:(c + 1) * P], hf[par][:, (4 * a + c) * P:(4 * a + c + 1) * P],
                                           ident[:])
                    ins.then_inc(hT_full, 1)

            def down_product(e, t, par, first):
                pe.wait_ge(h_low, t * 2 + 2)
                pe.wait_ge(stage_low, e * 4 + 4 * E + 4)
                if not first:
                    pe.wait_ge(y_done, t - 1)
                ins = three(j_bank[par][:, 0:D], [lambda a, fc=fc: hT[par][:, a, fc, :] for fc in range(FC)],
                            [lambda a, fc=fc: w2s[:, bass.ds(e, 1), a, fc, :].rearrange("p e d -> p (e d)") for fc in range(FC)])
                ins.then_inc(y_full, 1)

            pe.wait_ge(tables_done, 1)
            pe.wait_ge(stage_low, 4 * E)
            tile_T(0, 0, 0, 0, True)

            last_expert = [None]

            def step(t, par, buf, before, first, last):
                reload = last or (not isinstance(t, int) and buf == (2 + 1) % XG)
                e_before = expert(t - 1) if reload else last_expert[0]
                e = last_expert[0] = expert(t)
                if not last:
                    tile_T(t + 1, 1 - par, buf, before, first)
                up_product(e, t, par, first)
                if not first:
                    down_product(e_before, t - 1, 1 - par, isinstance(t, int) and t < 3)
                hidden_T(t, par, first)

            run_tiles(pe, step)
            down_product(last_expert[0], TILES - 1, (TILES - 1) % 2, False)


INPUTS = ("x", "ctxT", "wq", "wkv", "wo", "bo", "gx", "gf", "w1", "w2", "wr")


def kernel(x, ctx_1024, g_xattn, g_ffn, L0_xattn_w_q, L0_xattn_w_kv, L0_xattn_w_out, L0_xattn_b_out, L0_ffn_W1, L0_ffn_W2,
           L0_ffn_Wr):
    import concourse.bacc as bacc
    from concourse.bass_utils import run_bass_kernel_spmd

    def rows(a, k):
        return np.asarray(a).reshape(k, P, -1).transpose(1, 0, 2)

    layout = {
        "x": np.asarray(x).reshape(T, D),
        "ctxT": np.asarray(ctx_1024).reshape(B * M, KC, P).transpose(2, 1, 0),
        "wq": rows(L0_xattn_w_q, KC),
        "wkv": rows(L0_xattn_w_kv, KC),
        "wo": rows(L0_xattn_w_out, IC),
        "bo": np.asarray(L0_xattn_b_out),
        "gx": np.asarray(g_xattn),
        "gf": np.asarray(g_ffn),
        "w1": np.asarray(L0_ffn_W1).reshape(E, DFF, KC, P).transpose(0, 3, 2, 1),
        "w2": np.asarray(L0_ffn_W2).reshape(E, D, FC, P).transpose(0, 3, 2, 1),
        "wr": np.asarray(L0_ffn_Wr).reshape(E, KC, P).transpose(2, 1, 0),
    }
    nc = bacc.Bacc("TRN2", target_bir_lowering=False, num_devices=1)
    arrays = {f"in_{name}": np.ascontiguousarray(layout[name]) for name in INPUTS}
    args = [nc.dram_tensor(f"in_{name}", arrays[f"in_{name}"].shape, F32, kind="ExternalInput").ap() for name in INPUTS]
    out = nc.dram_tensor("out", (T + P, D), F32, kind="ExternalOutput").ap()
    xn2_dram = nc.dram_tensor("xn2", (T + P, D), F32, kind="Internal").ap()
    table = nc.dram_tensor("table", (P * (P + 1), 2), F32, kind="Internal").ap()
    build(nc, *args, out, xn2_dram, table)
    result = run_bass_kernel_spmd(nc, [arrays], core_ids=[0])
    return result.results[0]["out"][:T].reshape(B, N, D)
```

```python
from contextlib import ExitStack

import numpy as np

import concourse.bass as bass
from concourse import mybir

ALU = mybir.AluOpType
ACT = mybir.ActivationFunctionType
AX = mybir.AxisListType
F32 = mybir.dt.float32
F16 = mybir.dt.float16
I32 = mybir.dt.int32
U32 = mybir.dt.uint32
RMAX = bass.bass_isa.ReduceOp.max

P = 128
B, N, D = 8, 256, 256
M = 120
HEADS, DH = 16, 64
INNER = HEADS * DH
E, DFF = 8, 1024
T = B * N
KC = D // P
NT = N // P
TT = T // P
PAIRS = HEADS // 2
GH = 4
GROUPS = NT * HEADS // GH
IC = INNER // P
FC = DFF // P
TOPK = 2
TILES = TOPK * T // P + E - 1
BLOCKS = T // P
XG = 4
EPS = 1e-5
W2_EARLY, W2_LATE = (0, 1, 2, 3), (4, 6, 7, 5)
POOL_LOW = {4: 3, 5: 3, 6: 3}

UP_W = 2.0 ** 14
UP_X = 2.0 ** 10
DOWN_Q = 2.0 ** -18
DOWN_KV = 2.0 ** -23
UP_H = 2.0 ** 6
LN_UP_P = float(np.log(4096.0))
EXPONENT = 0x7F800000
UP_W_OVER = float((2 * 127 + 14) << 23)
RSQRT_MAGIC = float(0x5F3759DF)

JOBS = [
    (0, 1, "Ka", "n"),
    (1, 2, "Kb", "n"), (1, 2, "Va", "n"),
    (2, 0, "X2T0", "p"), (2, 1, "OT1a", "p"), (2, 1, "XT", "n"), (2, 1, "OT1b", "p"),
    (3, 1, "LG0", "p"), (3, 1, "Vb", "n"), (3, 2, "PJ1", "p"),
    (4, 0, "Q0", "n"), (4, 0, "RK0", "p"), (4, 1, "Q1", "n"), (4, 1, "Q2", "n"),
    (5, 2, "Q3", "n"),
    (6, 1, "X2T1", "p"), (6, 1, "OT0a", "c"), (6, 2, "LG1", "p"),
    (7, 0, "OT0b", "c"), (7, 0, "RK1", "p"), (7, 2, "PJ0", "c"),
]
NORM2_STEPS = (1, 4)
HIGH_STEPS = (0, 3, 3, 7)
SUM_STEPS = (3, 4, 5, 6)
ROUTE_STEPS = (4, 7)
PROLOGUE_JOBS = [(0, 0, n, "n") for n in ("XT", "Ka", "Kb", "Va", "Vb", "Q0", "Q1", "Q2", "Q3")]
EPILOGUE_JOBS = [(8, 0, "X2T0", "p"), (9, 0, "LG0", "p"), (9, 0, "OT1a", "p"), (9, 0, "OT1b", "p"), (10, 0, "RK0", "p"),
                 (10, 0, "PJ1", "p"), (11, 0, "X2T1", "p"), (12, 0, "LG1", "p"), (13, 0, "RK1", "p")]
JOB_BANKS = 3
HAS_HIGH = ("XT", "K", "V", "Q", "OT")


class Jobs:

    def __init__(self, jobs, k0, h0):
        self.at, self.steps, self.k0 = {}, {}, k0
        h = 0
        for i, (step, place, name, _) in enumerate(jobs):
            high = name.startswith(HAS_HIGH)
            job = (name, k0 + i, i % JOB_BANKS, h0 + h if high else None)
            self.at[name] = job
            self.steps.setdefault((step, place), []).append(job)
            h += high
        self.k_end, self.h_end = k0 + len(jobs), h0 + h

    def of(self, step, *places):
        return [j for p in places or (0,) for j in self.steps.get((step, p), [])]


def batch_jobs(b, prev, nxt):
    jobs = [j for j in JOBS if (j[3] != "p" or prev) and (j[3] != "n" or nxt)]
    if not prev:
        return Jobs(jobs, len(PROLOGUE_JOBS), len(PROLOGUE_JOBS))
    high = sum(j[2].startswith(HAS_HIGH) for j in JOBS)
    first = len(PROLOGUE_JOBS) + sum(j[3] != "p" for j in JOBS)
    first_high = len(PROLOGUE_JOBS) + sum(j[3] != "p" and j[2].startswith(HAS_HIGH) for j in JOBS)
    return Jobs(jobs, (b - 1) * len(JOBS) + first, (b - 1) * high + first_high)


def epilogue_jobs():
    last = batch_jobs(B - 1, True, False)
    return Jobs(EPILOGUE_JOBS, last.k_end, last.h_end)


def run_batches(eng, body):
    body(0, 0, False, True)
    with eng.Fori(0, (B - 2) // 2) as i:
        body(i * 2 + 1, 1, True, True)
        body(i * 2 + 2, 0, True, True)
    body(B - 1, (B - 1) % 2, True, False)


def run_tiles(eng, step):
    step(0, 0, 1, 0, True, False)
    step(1, 1, 2, 0, False, False)
    with eng.Fori(0, (TILES - 3) // XG) as i:
        for j in range(XG):
            step(i * XG + 2 + j, j % 2, (3 + j) % XG, i + (3 + j) // XG, False, False)
    step(TILES - 1, (TILES - 1) % 2, None, None, False, True)


class Chain:

    def __init__(self, eng, sem):
        self.eng, self.sem, self.base, self.n = eng, sem, 0, 0

    def link(self, ins, constant=None):
        self.n += 1
        ins.then_inc(self.sem, 1)
        count = self.base + self.n
        if constant is not None and not isinstance(count, int):
            count = self.eng.to_reg(count)
            self.eng.wait_ge(constant, 1)
        self.eng.wait_ge(self.sem, count)


def build(nc, x, ctxT, wq, wkv, wo, bo, gx, gf, w1, w2, wr, out, xn2_dram, table):
    ctx = ExitStack()
    with ctx:
        def sem(name):
            return ctx.enter_context(nc.semaphore(name))

        def sb(name, shape, dt, scope=ctx):
            return scope.enter_context(nc.sbuf_tensor(name, shape, dt))

        w1s = sb("w1s", [P, E, 2, KC, DFF], F16)
        stage = [sb(f"stage{i}", [P, 2048], F32) for i in range(2)]
        ident = sb("ident", [P, P], F32)
        upper = sb("upper", [P, P], F16)
        ones = sb("ones", [P, P], F16)
        iota8 = sb("iota8", [P, E], F32)
        token = sb("token", [P, TT], F32)
        seg = sb("seg", [P, E], F32)
        tg = sb("tg", [P, 2], F32)
        amax = sb("amax", [P, 4], F32)
        amax_all = sb("amax_all", [P, 4], F32)
        pw = sb("pw", [P, 4], F32)
        up = sb("up", [P, 4], F32)
        tmp = sb("tmp", [P, 8], F32)
        logit_scale = sb("logit_scale", [P, 1], F32)
        attn_scale = sb("attn_scale", [P, 1], F32)

        row_id = sb("row_id", [P, 1], F32)
        tile_id = sb("tile_id", [P, TILES + 1], F32)
        base = [sb(f"base{i}", [P, E], F32) for i in range(2)]
        amc = [sb(f"amc{i}", [P, 5], F32) for i in range(2)]
        amc_all = [sb(f"amc_all{i}", [P, 5], F32) for i in range(2)]
        pw1 = sb("pw1", [P, E], F32)
        pw2 = sb("pw2", [P, E], F32)
        upw = [sb(f"upw{i}", [P, 1], F32) for i in range(2)]
        amc2 = sb("amc2", [P, E, 5], F32)
        amc2_all = sb("amc2_all", [P, E, 5], F32)
        upw2 = sb("upw2", [P, E], F32)
        small8 = sb("small8", [P, 8, E], F32)
        small8i = sb("small8i", [P, 2, E], I32)
        blk = sb("blk", [P, 1], I32)
        expert_of = sb("expert_of", [P, TILES], I32)
        z_scale = sb("z_scale", [P, TILES], F32)
        h_scale = sb("h_scale", [P, TILES], F32)
        y_scale = sb("y_scale", [P, TILES], F32)
        row_of = sb("row_of", [P, TILES], I32)

        att = ctx.enter_context(ExitStack())
        wqs = sb("wqs", [P, 2, KC, INNER], F16, att)
        wkvs = sb("wkvs", [P, 2, KC, 2 * INNER], F16, att)
        ctxs = sb("ctxs", [P, 2, KC, B * M], F16, att)
        qT, kT, v = [None] * 2, [None] * 2, [None] * 2

        def heads(i):
            qT[i] = sb(f"qT{i}", [P, 2, PAIRS, N], F16, att)
            kT[i] = sb(f"kT{i}", [P, 2, PAIRS, 2 * M], F16, att)
            v[i] = sb(f"v{i}", [M, 2, HEADS, DH + 1], F16, att)

        heads(0)
        xin = sb("xin", [P, NT, D], F32, att)
        xn = sb("xn", [P, NT, D], F32, att)
        xnT = sb("xnT", [P, 2, KC, N], F16, att)
        taken = 4 * KC * (3 * INNER + B * M) + 4 * PAIRS * (N + 2 * M) + 4 * HEADS * (DH + 1) + 4 * NT * D + 4 * NT * D \
            + 4 * KC * N
        sb("gap", [P, E * 4 * DFF * KC - taken], mybir.dt.uint8, att)
        heads(1)
        wos = sb("wos", [P, 2, IC, D], F16, att)
        wrs = sb("wrs", [P, KC, E], F32, att)
        bout = sb("bout", [P, D], F32, att)
        xres = [sb(f"xres{i}", [P, D], F32, att) for i in range(2)]
        pr = [sb(f"pr{i}", [P, GH, M], F32, att) for i in range(2)]
        pT = [sb(f"pT{i}", [M, 2, GH, P], F16, att) for i in range(2)]
        o = [sb(f"o{i}", [P, INNER], F32, att) for i in range(2)]
        oT = sb("oT", [P, 2, IC, P], F16, att)
        x2 = [sb(f"x2_{i}", [P, D], F32, att) for i in range(2)]
        xn2 = [sb(f"xn2_{i}", [P, D], F32, att) for i in range(2)]
        xn2T = [sb(f"xn2T{i}", [P, KC, P], F32, att) for i in range(2)]
        stats = sb("stats", [P, TT, 6], F32, att)
        mv = sb("mv", [P, TT, 2], F32, att)
        ln_a = sb("ln_a", [P, 4, TT], F32, att)
        ln_scale = sb("ln_scale", [P, TT], F32, att)
        ln_shift = sb("ln_shift", [P, TT], F32, att)
        nmax = [sb(f"nmax{i}", [P, GH], F32, att) for i in range(2)]
        ebias = [sb(f"ebias{i}", [P, GH], F32, att) for i in range(2)]
        rsum = [sb(f"rsum{i}", [P, GH], F32, att) for i in range(2)]
        stats2 = [sb(f"stats2_{i}", [P, 6], F32, att) for i in range(2)]
        mv2 = [sb(f"mv2_{i}", [P, 2], F32, att) for i in range(2)]
        ln_b = [sb(f"ln_b{i}", [P, 6], F32, att) for i in range(2)]
        top = [sb(f"top{i}", [P, 8], F32, att) for i in range(2)]
        top_at = [sb(f"top_at{i}", [P, 8], U32, att) for i in range(2)]
        chosen = [sb(f"chosen{i}", [P, TOPK, E], F32, att) for i in range(2)]
        mask = [sb(f"mask{i}", [P, E], F16, att) for i in range(2)]
        slot_e = [sb(f"slot_e{i}", [P, E], F32, att) for i in range(2)]
        slot_m = [sb(f"slot_m{i}", [P, TOPK, E], F32, att) for i in range(2)]
        slot = [sb(f"slot{i}", [P, TOPK], I32, att) for i in range(2)]
        ratio = [sb(f"ratio{i}", [P, 2], F32, att) for i in range(2)]
        entry = [sb(f"entry{i}", [P, TOPK, 2], F32, att) for i in range(2)]
        pad = sb("pad", [P, P, 2], F32, att)
        att.close()

        w2s = sb("w2s", [P, E, 2, FC, D], F16)
        land = [sb(f"land{i}", [P, FC * D], F32) for i in range(2)]
        found = sb("found", [P, 2 * P], F32)
        by_expert = sb("by_expert", [P, TILES, E], F32)
        one_hot = sb("one_hot", [P, TILES, E], F32)
        expert_f = sb("expert_f", [P, TILES], F32)
        gate_y = sb("gate_y", [P, TILES], F32)
        xg = [sb(f"xg{i}", [P, D], F32) for i in range(XG)]
        xsT = [sb(f"xsT{i}", [P, 2, KC, P], F16) for i in range(2)]
        hf = [sb(f"hf{i}", [P, DFF], F32) for i in range(2)]
        hT = [sb(f"hT{i}", [P, 2, FC, P], F16) for i in range(2)]
        yt = [sb(f"yt{i}", [P, D], F32) for i in range(2)]

        raw = w1s[:].rearrange("p e s k f -> p (e s k f)").bitcast(F32)
        raw_kv = raw[:, 0:4096].rearrange("p (k n) -> p k n", k=KC)
        raw_q = raw[:, 4096:6144].rearrange("p (k n) -> p k n", k=KC)
        raw_o = raw[:, 6144:8192].rearrange("p (k n) -> p k n", k=IC)
        raw_ctx = raw[:, 8192:8192 + KC * B * M].rearrange("p (k n) -> p k n", k=KC)
        x_all = [s[:].rearrange("p (t d) -> p t d", d=D) for s in stage]

        def pb(name):
            return ctx.enter_context(nc.psum_tensor(name, [P, 512], F32))

        s_bank = [pb(f"s_bank{i}") for i in range(2)]
        t_bank = pb("t_bank")
        o_bank = [pb(f"o_bank{i}") for i in range(2)]
        j_bank = [pb(f"j_bank{i}") for i in range(JOB_BANKS)]
        z_bank, hT_bank = o_bank, [t_bank, j_bank[2]]

        const_done = sem("const_done")
        raw_in = [sem(f"raw_in{i}") for i in range(4)]
        small_in = sem("small_in")
        x_all_in = [sem(f"x_all_in{i}") for i in range(2)]
        xin_in = sem("xin_in")
        xres_in = [sem(f"xres_in{i}") for i in range(NT)]
        zero_done = sem("zero_done")
        amax_done = sem("amax_done")
        allmax_done = sem("allmax_done")
        scales_done = sem("scales_done")
        tanh_done = sem("tanh_done")
        router_scaled = sem("router_scaled")
        w_high = sem("w_high")
        w_low = sem("w_low")
        dve_chain = sem("dve_chain")
        pool_chain = sem("pool_chain")
        xn_done = sem("xn_done")
        job_full = sem("job_full")
        job_high = sem("job_high")
        job_free = sem("job_free")
        scores_full = sem("scores_full")
        bias_done = sem("bias_done")
        exp_done = sem("exp_done")
        pT_full = sem("pT_full")
        pT_high = sem("pT_high")
        pT_low = sem("pT_low")
        av_full = sem("av_full")
        norm_done = sem("norm_done")
        xb_done = sem("xb_done")
        spare_zero = sem("spare_zero")
        xn2_out = [sem(f"xn2_out{i}") for i in range(NT)]
        ln2_start = sem("ln2_start")
        ln2_done = sem("ln2_done")
        xn2_done = sem("xn2_done")
        mask_done = sem("mask_done")
        ratio_done = sem("ratio_done")
        route_done = sem("route_done")
        table_in = sem("table_in")
        scattered = sem("scattered")
        slots_free = sem("slots_free")
        stage_in = [sem(f"stage_in{i}") for i in range(2)]
        amc_done = sem("amc_done")
        amc_reduced = sem("amc_reduced")
        upw_done = sem("upw_done")
        stage_high = sem("stage_high")
        stage_low = sem("stage_low")
        w2_in = [sem(f"w2_in{e}") for e in range(E)]
        amc_summed = sem("amc_summed")
        amc_maxed = sem("amc_maxed")
        w2_low_pool = sem("w2_low_pool")
        blk_done = sem("blk_done")
        found_in = sem("found_in")
        found_T = sem("found_T")
        tables_done = sem("tables_done")
        rows_done = sem("rows_done")
        xg_in = [sem(f"xg_in{i}") for i in range(XG)]
        xs_full = sem("xs_full")
        xs_high = sem("xs_high")
        xs_low = sem("xs_low")
        z_full = sem("z_full")
        hT_full = sem("hT_full")
        silu_done = sem("silu_done")
        h_high = sem("h_high")
        h_low = sem("h_low")
        y_full = sem("y_full")
        y_done = sem("y_done")
        y_added = sem("y_added")
        x2_out = [sem(f"x2_out{i}") for i in range(NT)]

        x_v = x.rearrange("(t p) d -> p t d", p=P)
        x_b = x.rearrange("(b t p) d -> b p t d", t=NT, p=P)
        out_t = out.rearrange("(t p) d -> t p d", p=P)
        x_t = x.rearrange("(t p) d -> t p d", p=P)
        xn2_t = xn2_dram.rearrange("(t p) d -> t p d", p=P)
        table_b = table.rearrange("(b r) c -> b (r c)", r=P)
        w1_v = w1.rearrange("e p k f -> e p (k f)")
        w2_v = w2.rearrange("e p c d -> e p (c d)")

        def w1_part(e, part, c):
            return w1s[:, bass.ds(e, 1), part].rearrange("p e k f -> p (e k f)")[:, c:c + 512]

        def w2_part(e, part, c):
            return w2s[:, e, part].rearrange("p c d -> p (c d)")[:, c:c + 512]

        w2_raw = [w2s[:, 4 + e].rearrange("p s c d -> p (s c d)").bitcast(F32) for e in range(4)]
        w2_raw += [t[:] for t in (*stage, *land)]

        SPLITS = ((raw_ctx, ctxs, 0), (raw_kv, wkvs, 1), (raw_q, wqs, 2), (raw_o, wos, 3))

        block = ctx.enter_context(nc.Block())

        @block.sync
        def _(sp):
            for i in range(2):
                sp.dma_start(x_all[i], x_v[:, 8 * i:8 * i + 8, :]).then_inc(x_all_in[i], 16)
            sp.dma_start(raw_ctx, ctxT).then_inc(raw_in[0], 16)
            sp.dma_start(raw_kv, wkv).then_inc(raw_in[1], 16)
            sp.dma_start(raw_q, wq).then_inc(raw_in[2], 16)
            sp.dma_start(raw_o, wo).then_inc(raw_in[3], 16)

            sp.wait_ge(spare_zero, 1)
            sp.dma_start(out[T:T + P, :], x2[1][:]).then_inc(x2_out[1], 16)
            for i in range(2):
                sp.dma_start(xn2_dram[T + 64 * i:T + 64 * i + 64, :], x2[1][64 * i:64 * i + 64, :]).then_inc(xn2_out[i], 16)
            sp.wait_ge(const_done, 9)
            sp.dma_start(table_b[0:P, :], pad[:].rearrange("p r c -> p (r c)")).then_inc(table_in, 16)
            sp.dma_start(table_b[P:P + 1, :], pad[0:1].rearrange("p r c -> p (r c)")).then_inc(table_in, 16)
            sp.wait_ge(xn_done, 1)
            sp.dma_start(stage[0][:], w1_v[0]).then_inc(stage_in[0], 16)

            def store(b, nt):
                sp.dma_start(out_t[bass.ds(b * 2 + nt, 1)].rearrange("a p d -> p (a d)"), x2[nt][:]).then_inc(x2_out[nt], 16)

            def store_norm(b, nt):
                sp.wait_ge(xn2_done, b * 2 + nt + 1)
                sp.dma_start(xn2_t[bass.ds(b * 2 + nt, 1)].rearrange("a p d -> p (a d)"), xn2[nt][:]).then_inc(xn2_out[nt], 16)

            def body(b, parity, prev, nxt):
                jobs = batch_jobs(b, prev, nxt)
                if prev:
                    sp.wait_ge(job_free, jobs.k0)
                    store(b - 1, 0)
                sp.dma_start(xres[0][:], x_t[bass.ds(b * 2, 1)].rearrange("a p d -> p (a d)")).then_inc(xres_in[0], 16)
                if prev:
                    store_norm(b - 1, 0)
                    sp.wait_ge(job_free, jobs.at["PJ1"][1] + 1)
                    store(b - 1, 1)
                if not nxt:
                    for e in range(4):
                        sp.dma_start(w2_raw[e], w2_v[e]).then_inc(w2_in[e], 16)
                sp.dma_start(xres[1][:], x_t[bass.ds(b * 2 + 1, 1)].rearrange("a p d -> p (a d)")).then_inc(xres_in[1], 16)
                if prev:
                    store_norm(b - 1, 1)
                    sp.wait_ge(stage_low, b * 4)
                if nxt:
                    sp.dma_start(stage[1 - parity][:], w1_v[bass.ds(b + 1, 1)].rearrange("a p n -> p (a n)")).then_inc(
                        stage_in[1 - parity], 16)
                else:
                    sp.dma_start(w2_raw[4], w2_v[4]).then_inc(w2_in[4], 16)

            run_batches(sp, body)
            sp.wait_ge(job_free, epilogue_jobs().k0)
            store(B - 1, 0)
            store_norm(B - 1, 0)
            sp.wait_ge(job_free, epilogue_jobs().at["PJ1"][1] + 1)
            store(B - 1, 1)
            store_norm(B - 1, 1)
            sp.wait_ge(norm_done, B * GROUPS)
            for e in (6, 7):
                sp.dma_start(w2_raw[e], w2_v[e]).then_inc(w2_in[e], 16)
            sp.wait_ge(stage_low, 4 * E)
            sp.dma_start(w2_raw[5], w2_v[5]).then_inc(w2_in[5], 16)
            sp.wait_ge(x2_out[0], 16 * B)
            sp.wait_ge(x2_out[1], 16 * (B + 1))

        @block.gpsimd
        def _(pool):
            def load_x(b):
                if b:
                    pool.wait_ge(xn_done, b)
                pool.dma_start(xin[:], x_b[b]).then_inc(xin_in, 16)

            load_x(0)
            pool.memset(ident[:], 0.0).then_inc(pool_chain, 1)
            pool.memset(upper[:], 1.0).then_inc(pool_chain, 1)
            pool.memset(ones[:], 1.0).then_inc(const_done, 1)
            pool.iota(iota8[:], [[1, E]], base=0, channel_multiplier=0,
                      allow_small_or_imprecise_dtypes=True).then_inc(const_done, 1)
            pool.iota(token[:], [[P, TT]], base=0, channel_multiplier=1,
                      allow_small_or_imprecise_dtypes=True).then_inc(const_done, 1)
            pool.iota(seg[:], [[T, E]], base=0, channel_multiplier=0,
                      allow_small_or_imprecise_dtypes=True).then_inc(const_done, 1)
            pool.iota(row_id[:], [[0, 1]], base=0, channel_multiplier=1,
                      allow_small_or_imprecise_dtypes=True).then_inc(const_done, 1)
            pool.iota(tile_id[:], [[1, TILES + 1]], base=0, channel_multiplier=0,
                      allow_small_or_imprecise_dtypes=True).then_inc(const_done, 1)
            pool.memset(pad[:], 0.0).then_inc(pool_chain, 1)
            pool.wait_ge(pool_chain, 3)
            pool.iota(pad[:, :, 0], [[1, P]], base=T, channel_multiplier=0,
                      allow_small_or_imprecise_dtypes=True).then_inc(const_done, 1)
            pool.affine_select(out=ident[:], in_=ident[:], compare_op=ALU.not_equal, fill=1.0, base=0,
                               pattern=[[-1, P]], channel_multiplier=1).then_inc(const_done, 1)
            pool.affine_select(out=upper[:], in_=upper[:], compare_op=ALU.is_gt, fill=0.0, base=0,
                               pattern=[[1, P]], channel_multiplier=-1).then_inc(const_done, 1)
            pool.wait_ge(amax_done, 4)
            pool.partition_all_reduce(amax_all[:], amax[:], P, RMAX).then_inc(allmax_done, 1)

            load_x(1)
            pool.sem_inc(slots_free, 1)

            chain = Chain(pool, pool_chain)
            chain.base = 3

            def residual(m):
                pool.wait_ge(xres_in[m % 2], 16 * (m // 2 + 1))
                if m == 0:
                    pool.wait_ge(tanh_done, 2)
                pool.tensor_tensor(xres[m % 2][:], xres[m % 2][:], bout[:], ALU.add).then_inc(xb_done, 1)

            def norm_scale(m):
                c, y, a, sc, sh = (ln_b[m % 2][:, k:k + 1] for k in (0, 1, 2, 3, 4))
                pool.wait_ge(ln2_start, m + 1)
                for _ in range(3):
                    chain.link(pool.tensor_scalar(a, y, y, c, ALU.mult, ALU.mult))
                    chain.link(pool.tensor_scalar(a, a, -0.5, 1.5, ALU.mult, ALU.add))
                    chain.link(pool.tensor_tensor(y, y, a, ALU.mult))
                chain.link(pool.tensor_scalar(sc, y, UP_X, None, ALU.mult))
                chain.link(pool.tensor_scalar(a, mv2[m % 2][:, 0:1], -1.0, None, ALU.mult))
                pool.tensor_tensor(sh, a, sc, ALU.mult).then_inc(ln2_done, 1)

            def scatter(m):
                pool.wait_ge(route_done, m + 1)
                if m == 0:
                    pool.wait_ge(table_in, 32)
                for k in range(TOPK):
                    if m or k:
                        pool.wait_ge(scattered, 16 * (m * TOPK + k))
                    if k == 0:
                        pool.sem_inc(slots_free, 1)
                    pool.indirect_dma_start(out=table[:], out_offset=bass.IndirectOffsetOnAxis(slot[m % 2][:, k:k + 1], 0),
                                            in_=entry[m % 2][:, k, :], in_offset=None).then_inc(scattered, 16)

            def reduce_stage(q):
                pool.wait_ge(amc_done, q + 1)
                pool.partition_all_reduce(amc_all[q % 2][:], amc[q % 2][:], P, RMAX).then_inc(amc_reduced, 1)

            def split_low(q, chunks):
                for k in chunks:
                    pool.wait_ge(stage_high, 4 * q + k + 1)
                    c = 512 * k
                    chunk = stage[q % 2][:, c:c + 512]
                    chain.link(pool.tensor_scalar(chunk, chunk, upw[q % 2][:], None, ALU.mult))
                    pool.tensor_tensor(w1_part(q, 1, c), chunk, w1_part(q, 0, c), ALU.subtract).then_inc(stage_low, 1)

            def reduce_w2(late):
                g = slice(4 * late, 4 * late + 4)
                if not late:
                    pool.wait_ge(amc_maxed, 1)
                pool.wait_ge(amc_summed, 1 + late)
                pool.partition_all_reduce(amc2_all[:, g].rearrange("p e k -> p (e k)"), amc2[:, g].rearrange("p e k -> p (e k)"),
                                          P, RMAX).then_inc(amc_reduced, 1)

            for b in range(B + 1):
                if b < B:
                    residual(2 * b)
                if 0 < b < B:
                    split_low(b - 1, (0,))
                if b == B:
                    reduce_w2(False)
                if b:
                    norm_scale(2 * b - 1)
                if b + 2 < B:
                    load_x(b + 2)
                if 0 < b < B:
                    split_low(b - 1, (1,))
                if b < B:
                    reduce_stage(b)
                if b:
                    scatter(2 * b - 2)
                if 0 < b < B:
                    split_low(b - 1, (2, 3))
                if b < B:
                    residual(2 * b + 1)
                    norm_scale(2 * b)
                if b:
                    scatter(2 * b - 1)

            pool.wait_ge(blk_done, 1)
            pool.wait_ge(scattered, 16 * TT * TOPK)
            pool.indirect_dma_start(out=found[0:TILES, :], out_offset=None, in_=table_b,
                                    in_offset=bass.IndirectOffsetOnAxis(blk[0:TILES, :], 0)).then_inc(found_in, 16)
            reduce_w2(True)

            def gather(t):
                if t >= XG:
                    pool.wait_ge(xs_full, t - XG + 1)
                pool.indirect_dma_start(out=xg[t % XG][:], out_offset=None, in_=xn2_dram[:],
                                        in_offset=bass.IndirectOffsetOnAxis(row_of[:, t:t + 1], 0)).then_inc(xg_in[t % XG], 16)

            pool.wait_ge(rows_done, 1)
            for i in range(NT):
                pool.wait_ge(xn2_out[i], 16 * (B + 1))
                pool.wait_ge(x2_out[i], 16 * (B + i))
            for t in range(XG):
                gather(t)
            for e, first in POOL_LOW.items():
                for k in range(first, 4):
                    pool.wait_ge(stage_high, 4 * (E + e) + k + 1)
                    chunk = w2_raw[e][:, 512 * k:512 * k + 512]
                    chain.link(pool.tensor_scalar(chunk, chunk, upw2[:, e:e + 1], None, ALU.mult))
                    pool.tensor_tensor(w2_part(e, 1, 512 * k), chunk, w2_part(e, 0, 512 * k),
                                       ALU.subtract).then_inc(w2_low_pool, 1)
            for t in range(TILES):
                if t and t + XG - 1 < TILES:
                    gather(t + XG - 1)
                pool.wait_ge(y_done, t + 1)
                if t:
                    pool.wait_ge(y_added, 16 * t)
                pool.indirect_dma_start(out=out[:], out_offset=bass.IndirectOffsetOnAxis(row_of[:, t:t + 1], 0),
                                        in_=yt[t % 2][:], in_offset=None, compute_op=ALU.add).then_inc(y_added, 16)
            pool.wait_ge(y_added, 16 * TILES)

        @block.scalar
        def _(act):
            act.dma_start(tg[:, 0:1], gx.unsqueeze(0).to_broadcast((P, 1))).then_inc(small_in, 16)
            act.dma_start(tg[:, 1:2], gf.unsqueeze(0).to_broadcast((P, 1))).then_inc(small_in, 16)
            act.dma_start(bout[:], bo.unsqueeze(0).to_broadcast((P, D))).then_inc(small_in, 16)
            act.dma_start(wrs[:], wr).then_inc(small_in, 16)
            act.wait_ge(small_in, 64)
            nc.scalar.activation(wrs[:], wrs[:], ACT.Copy, scale=1.0 / UP_X).then_inc(router_scaled, 1)
            nc.scalar.activation(tg[:], tg[:], ACT.Tanh).then_inc(tanh_done, 1)
            act.wait_ge(scales_done, 1)
            for src, dst, i in SPLITS:
                for k in range(src.shape[1]):
                    nc.scalar.activation(dst[:, 0, k, :], src[:, k, :], ACT.Copy,
                                         scale=up[:, i:i + 1]).then_inc(w_high, 1)

            def job(j, par):
                name, k, bank, h = j
                src = j_bank[bank]
                if h is None:
                    return
                act.wait_ge(job_full, k + 1)
                if name == "XT":
                    nc.scalar.activation(xnT[:, 0].rearrange("p k n -> p (k n)"), src[:], ACT.Copy).then_inc(job_high, 1)
                elif name[0] == "K":
                    c = 4 * (name == "Kb")
                    for a in range(2):
                        ins = nc.scalar.activation(kT[par][64 * a:64 * a + 64, 0, c:c + 4, a * M:a * M + M],
                                                   src[64 * a:64 * a + 64, 0:4 * M].rearrange("p (c m) -> p c m", m=M),
                                                   ACT.Copy, scale=DOWN_KV)
                    ins.then_inc(job_high, 1)
                elif name[0] == "V":
                    c = 8 * (name == "Vb")
                    nc.scalar.activation(v[par][:, 0, c:c + 8, 0:DH], src[0:M, :].rearrange("p (h d) -> p h d", d=DH),
                                         ACT.Copy, scale=DOWN_KV).then_inc(job_high, 1)
                elif name[0] == "Q":
                    c = 2 * int(name[1])
                    nc.scalar.activation(qT[par][:, 0, c:c + 2, :], src[:].rearrange("p (c n) -> p c n", c=2),
                                         ACT.Copy, scale=DOWN_Q).then_inc(job_high, 1)
                else:
                    c = 4 * (name[3] == "b")
                    nc.scalar.activation(oT[:, 0, c:c + 4, :], src[:].rearrange("p (c n) -> p c n", c=4),
                                         ACT.Copy).then_inc(job_high, 1)

            def pT_split(g, s):
                act.wait_ge(pT_full, g + 1)
                nc.scalar.activation(pT[s % 2][:, 0], t_bank[0:M, :].rearrange("p (h n) -> p h n", h=GH),
                                     ACT.Copy).then_inc(pT_high, 1)

            def exps(g, s, prev):
                act.wait_ge(bias_done, g + 1)
                if prev or s >= 2:
                    act.wait_ge(pT_full, g - 1)
                for h in range(GH):
                    ins = nc.scalar.activation(pr[s % 2][:, h, :], s_bank[s % 2][:, h * M:(h + 1) * M], ACT.Exp,
                                               bias=ebias[s % 2][:, h:h + 1], scale=logit_scale[:])
                ins.then_inc(exp_done, 1)

            for j in Jobs(PROLOGUE_JOBS, 0, 0).of(0):
                job(j, 0)

            def gate_ratio(b, nt):
                act.wait_ge(mask_done, b * 2 + nt + 1)
                nc.scalar.activation(ratio[nt][:, 0:1], top[nt][:, 0:1], ACT.Exp, bias=top[nt][:, 1:2],
                                     scale=-1.0).then_inc(ratio_done, 1)

            def norm_x(b):
                count = (b + 1) * 16 if isinstance(b, int) else act.to_reg((b + 1) * 16)
                act.wait_ge(xn_done, 1)
                act.wait_ge(xin_in, count)
                for t in range(NT):
                    ins = nc.scalar.activation(xn[:, t, :], xin[:, t, :], ACT.Identity, scale=ln_scale[:, bass.ds(b * 2 + t, 1)],
                                               bias=ln_shift[:, bass.ds(b * 2 + t, 1)])
                ins.then_inc(xn_done, 1)

            def norm2(b, nt):
                act.wait_ge(ln2_done, b * 2 + nt + 1)
                act.wait_ge(xn2_out[nt], b * 16 + 16)
                nc.scalar.activation(xn2[nt][:], x2[nt][:], ACT.Identity, scale=ln_b[nt][:, 3:4],
                                     bias=ln_b[nt][:, 4:5]).then_inc(xn2_done, 1)

            def stage_sum(q, par, k):
                if k == 0:
                    act.wait_ge(stage_in[par], q // 2 * 16 + 16 if isinstance(q, int) else (q - par) * 8 + 16)
                c = 512 * k
                ins = nc.scalar.activation(w1_part(q, 0, c), stage[par][:, c:c + 512], ACT.Abs, accum_out=amc[par][:, k:k + 1])
                if k == 3:
                    ins.then_inc(amc_done, 1)

            def split_high(q, par, k):
                if k == 0:
                    count = q + 1 if isinstance(q, int) else act.to_reg(q + 1)
                    act.wait_ge(xn_done, 1)
                    act.wait_ge(upw_done, count)
                c = 512 * k
                nc.scalar.activation(w1_part(q, 0, c), stage[par][:, c:c + 512], ACT.Copy,
                                     scale=upw[par][:]).then_inc(stage_high, 1)

            def w2_sums(experts, chunks, done, junk):
                for n, e in enumerate(experts):
                    act.wait_ge(w2_in[e], 16)
                    for k in chunks:
                        ins = nc.scalar.activation(junk(len(chunks) * n + k - chunks[0]), w2_raw[e][:, 512 * k:512 * k + 512], ACT.Abs,
                                                   accum_out=amc2[:, e, k:k + 1])
                if done:
                    ins.then_inc(amc_summed, 1)

            def w2_high(e):
                act.wait_ge(upw_done, E + 1 + e // 4)
                if e >= 4:
                    act.wait_ge(stage_low, (E + e - 3) * 4)
                for k in range(4):
                    c = 512 * k
                    nc.scalar.activation(w2_part(e, 0, c), w2_raw[e][:, c:c + 512], ACT.Copy,
                                         scale=upw2[:, e:e + 1]).then_inc(stage_high, 1)

            def body(b, parity, prev, nxt):
                jobs = batch_jobs(b, prev, nxt)
                for s in range(GROUPS):
                    exps(b * 8 + s, s, prev)
                    if s == 0 and nxt:
                        norm_x(b + 1)
                    for j in jobs.of(s, 0):
                        job(j, 1 - parity)
                    if prev or s >= 1:
                        pT_split(b * 8 + s - 1, s - 1)
                    for j in jobs.of(s, 1, 2):
                        job(j, 1 - parity)
                    if prev and s in (3, 7):
                        gate_ratio(b - 1, s // 4)
                    if prev and s in NORM2_STEPS:
                        norm2(b - 1, NORM2_STEPS.index(s))
                    for k in range(4):
                        if prev and s == HIGH_STEPS[k]:
                            split_high(b - 1, 1 - parity, k)
                    for k in range(4):
                        if s == SUM_STEPS[k]:
                            stage_sum(b, parity, k)

            run_batches(act, body)
            jobs = epilogue_jobs()
            pT_split(8 * B - 1, 7)
            norm2(B - 1, 0)
            for s in range(8, 14):
                if s == 11:
                    norm2(B - 1, 1)
                for j in jobs.of(s):
                    job(j, 0)
                if s in (10, 13):
                    gate_ratio(B - 1, int(s == 13))
                if s < 12:
                    split_high(B - 1, 1, s - 8)
                if s == 9:
                    w2_sums(W2_LATE[:1], range(4), False, lambda n: w2_part(n // 2, 0, 512 * (2 + n % 2)))
                    w2_sums(W2_EARLY, (2, 3), True, lambda n: w2_part(n // 2, 0, 512 * (n % 2)))
                if s in (11, 12):
                    w2_high(W2_EARLY[s - 11])
            spare = [t[:].rearrange("p a c n -> p (a c n)") for t in hT] + [t[:].bitcast(F16) for t in hf]
            spare = [t[:, 512 * k:512 * k + 512] for t in spare for k in range(4)]
            for e in W2_EARLY[2:]:
                w2_high(e)
            w2_sums(W2_LATE[1:], range(4), True, lambda n: spare[n])
            w2_high(4)

            def x_high(t, par, first):
                act.wait_ge(xs_full, t + 1)
                if not first:
                    act.wait_ge(z_full, t * 2 - 2)
                nc.scalar.activation(xsT[par][:, 0].rearrange("p k n -> p (k n)"), s_bank[par][:, 0:D],
                                     ACT.Copy).then_inc(xs_high, 1)

            def later(sem, t, a):
                count = t * 2 + a + 1 if isinstance(t, int) else act.to_reg(t * 2 + a + 1)
                act.wait_ge(tables_done, 1)
                act.wait_ge(sem, count)

            def silu(t, par):
                for a in range(2):
                    later(z_full, t, a)
                    nc.scalar.activation(hf[par][:, 512 * a:512 * a + 512], z_bank[a][:], ACT.Silu,
                                         scale=z_scale[:, bass.ds(t, 1)]).then_inc(silu_done, 1)

            def h_split(t, par):
                for a in range(2):
                    later(hT_full, t, a)
                    nc.scalar.activation(hT[par][:, 0, 4 * a:4 * a + 4, :], hT_bank[a][:].rearrange("p (c n) -> p c n", c=4),
                                         ACT.Copy, scale=h_scale[:, bass.ds(t, 1)]).then_inc(h_high, 1)

            act.wait_ge(tables_done, 1)
            x_high(0, 0, True)

            def step(t, par, buf, before, first, last):
                if not last:
                    x_high(t + 1, 1 - par, first)
                if first:
                    w2_high(5)
                    w2_high(6)
                silu(t, par)
                h_split(t, par)
                if first:
                    w2_high(7)

            run_tiles(act, step)

        @block.vector
        def _(dve):
            chain = Chain(dve, dve_chain)

            for i in range(2):
                for h in range(2):
                    nc.vector.memset(kT[i][64:128, h, :, 0:M], 0.0)
                    nc.vector.memset(kT[i][0:64, h, :, M:2 * M], 0.0)
                    nc.vector.memset(v[i][:, h, :, DH:DH + 1], 1.0 - h).then_inc(zero_done, 1)
            nc.vector.memset(x2[1][:], 0.0).then_inc(spare_zero, 1)
            for i in range(2):
                nc.vector.memset(amc[i][:, 4:5], 1e-30)
            nc.vector.memset(amc2[:, :, 4:5], 1e-30)
            dve.wait_ge(const_done, 9)
            chain.link(nc.vector.tensor_copy(base[0][:], seg[:]))
            for t in range(TT):
                if t % 8 == 0:
                    dve.wait_ge(x_all_in[t // 8], 16)
                ins = nc.vector.bn_stats(stats[:, t, :], x_all[t // 8][:, t % 8, :])
            chain.link(ins)
            for t in range(TT):
                ins = nc.vector.bn_aggr(mv[:, t, :], stats[:, t, :])
            chain.link(ins)

            def rsqrt(var, y, a, c):
                chain.link(nc.vector.tensor_scalar(c, var, EPS, None, ALU.add))
                chain.link(nc.vector.tensor_scalar(a.bitcast(U32), c.bitcast(U32), 1, None, ALU.logical_shift_right))
                chain.link(nc.vector.tensor_scalar(y.bitcast(I32), a.bitcast(I32), -1.0, RSQRT_MAGIC, ALU.mult, ALU.add))
                for _ in range(3):
                    chain.link(nc.vector.tensor_tensor(a, y, y, ALU.mult))
                    chain.link(nc.vector.tensor_tensor(a, a, c, ALU.mult))
                    chain.link(nc.vector.tensor_scalar(a, a, -0.5, 1.5, ALU.mult, ALU.add))
                    chain.link(nc.vector.tensor_tensor(y, y, a, ALU.mult))

            rsqrt(mv[:, :, 1], ln_a[:, 0, :], ln_a[:, 1, :], ln_a[:, 2, :])
            chain.link(nc.vector.tensor_scalar(ln_scale[:], ln_a[:, 0, :], UP_X, None, ALU.mult))
            chain.link(nc.vector.scalar_tensor_tensor(out=ln_shift[:], in0=mv[:, :, 0], scalar=-1.0, in1=ln_scale[:],
                                                      op0=ALU.mult, op1=ALU.mult))

            dve.wait_ge(xin_in, 16)
            for t in range(NT):
                ins = nc.vector.tensor_scalar(xn[:, t, :], xin[:, t, :], ln_scale[:, t:t + 1], ln_shift[:, t:t + 1],
                                              ALU.mult, ALU.add)
            ins.then_inc(xn_done, 1)
            for i, (src, _, _) in enumerate(SPLITS):
                dve.wait_ge(raw_in[i], 16)
                nc.vector.tensor_reduce(amax[:, i:i + 1], src.rearrange("p k n -> p (k n)"), AX.X, ALU.max,
                                        apply_absolute_value=True).then_inc(amax_done, 1)
            dve.wait_ge(allmax_done, 1)
            chain.link(nc.vector.tensor_scalar(pw[:], amax_all[:], 1e-30, None, ALU.max))
            chain.link(nc.vector.tensor_scalar(pw[:].bitcast(U32), pw[:].bitcast(U32), EXPONENT, None, ALU.bitwise_and))
            chain.link(nc.vector.reciprocal(up[:], pw[:]))
            chain.link(nc.vector.tensor_scalar(up[:], up[:], UP_W, None, ALU.mult))
            chain.link(nc.vector.tensor_tensor(tmp[:, 0:1], pw[:, 0:1], pw[:, 1:2], ALU.mult))
            chain.link(nc.vector.scalar_tensor_tensor(out=logit_scale[:], in0=tmp[:, 0:1], scalar=2.0 ** -14,
                                                      in1=pw[:, 2:3], op0=ALU.mult, op1=ALU.mult))
            dve.wait_ge(tanh_done, 1)
            chain.link(nc.vector.scalar_tensor_tensor(out=tmp[:, 1:2], in0=tmp[:, 0:1], scalar=2.0 ** -19,
                                                      in1=pw[:, 3:4], op0=ALU.mult, op1=ALU.mult))
            chain.link(nc.vector.tensor_tensor(attn_scale[:], tmp[:, 1:2], tg[:, 0:1], ALU.mult))
            nc.vector.tensor_scalar(bout[:], bout[:], tg[:, 0:1], None, ALU.mult).then_inc(tanh_done, 1)
            nc.vector.tensor_scalar(tmp[:, 2:3], up[:, 0:1], 1.0, None, ALU.mult).then_inc(scales_done, 1)
            n = 0
            for src, dst, i in SPLITS:
                for k in range(src.shape[1]):
                    n += 1
                    dve.wait_ge(w_high, n)
                    nc.vector.scalar_tensor_tensor(out=dst[:, 1, k, :], in0=src[:, k, :], scalar=up[:, i:i + 1],
                                                   in1=dst[:, 0, k, :], op0=ALU.mult,
                                                   op1=ALU.subtract).then_inc(w_low, 1)

            def low(dst, src, high, scale, inc):
                if scale == 1.0:
                    ins = nc.vector.tensor_tensor(dst, src, high, ALU.subtract)
                else:
                    ins = nc.vector.scalar_tensor_tensor(out=dst, in0=src, scalar=scale, in1=high,
                                                         op0=ALU.mult, op1=ALU.subtract)
                if inc is not None:
                    ins.then_inc(inc, 1)

            def job(j, par, b, prev_b, first=False):
                name, k, bank, h = j
                src = j_bank[bank]
                if h is not None:
                    dve.wait_ge(job_high, h + 1)
                elif name[:2] != "LG":
                    dve.wait_ge(job_full, k + 1)
                if name == "XT":
                    low(xnT[:, 1].rearrange("p k n -> p (k n)"), src[:], xnT[:, 0].rearrange("p k n -> p (k n)"), 1.0, job_free)
                elif name[0] == "K":
                    c = 4 * (name == "Kb")
                    for a in range(2):
                        r, cols = slice(64 * a, 64 * a + 64), slice(a * M, a * M + M)
                        low(kT[par][r, 1, c:c + 4, cols], src[r, 0:4 * M].rearrange("p (c m) -> p c m", m=M),
                            kT[par][r, 0, c:c + 4, cols], DOWN_KV, job_free if a else None)
                elif name[0] == "V":
                    c = 8 * (name == "Vb")
                    low(v[par][:, 1, c:c + 8, 0:DH], src[0:M, :].rearrange("p (h d) -> p h d", d=DH),
                        v[par][:, 0, c:c + 8, 0:DH], DOWN_KV, job_free)
                elif name[0] == "Q":
                    c = 2 * int(name[1])
                    low(qT[par][:, 1, c:c + 2, :], src[:].rearrange("p (c n) -> p c n", c=2),
                        qT[par][:, 0, c:c + 2, :], DOWN_Q, job_free)
                elif name[:2] == "OT":
                    c = 4 * (name[3] == "b")
                    low(oT[:, 1, c:c + 4, :], src[:].rearrange("p (c n) -> p c n", c=4), oT[:, 0, c:c + 4, :], 1.0, job_free)
                elif name[:2] == "PJ":
                    nt = int(name[2])
                    mb = (prev_b if nt else b) * 2 + nt
                    dve.wait_ge(xb_done, mb + 1)
                    if nt:
                        dve.wait_ge(x2_out[1], prev_b * 16 + 16)
                    elif not first:
                        dve.wait_ge(x2_out[0], b * 16)
                    nc.vector.scalar_tensor_tensor(out=x2[nt][:], in0=src[:, 0:D], scalar=attn_scale[:], in1=xres[nt][:],
                                                   op0=ALU.mult, op1=ALU.add).then_inc(job_free, 1)
                    dve.wait_ge(job_free, k + 1)
                    norm2_start(nt)
                elif name[:3] == "X2T":
                    nc.vector.tensor_copy(xn2T[int(name[3])][:].rearrange("p k n -> p (k n)"), src[:, 0:D]).then_inc(job_free, 1)
                elif name[:2] == "LG":
                    nt = int(name[2])
                    count = k + 1 if isinstance(k, int) else dve.to_reg(k + 1)
                    dve.wait_ge(const_done, 1)
                    dve.wait_ge(job_full, count)
                    choose(nt, src[:, 0:E])
                    choose_masks(nt, k)
                else:
                    nt = int(name[2])
                    chain.link(nc.vector.tensor_tensor(slot_e[nt][:], src[:, 0:E], base[nt][:], ALU.add))
                    nc.vector.tensor_tensor(base[1 - nt][:], src[:, E:2 * E], base[nt][:], ALU.add).then_inc(job_free, 1)

            def norm2_start(nt):
                c, y = (ln_b[nt][:, k:k + 1] for k in range(2))
                chain.link(nc.vector.bn_stats(stats2[nt][:], x2[nt][:]), const_done)
                chain.link(nc.vector.bn_aggr(mv2[nt][:], stats2[nt][:]))
                chain.link(nc.vector.tensor_scalar(c, mv2[nt][:, 1:2], EPS, None, ALU.add))
                nc.vector.tensor_scalar(y.bitcast(I32), c.bitcast(I32), -0.5, RSQRT_MAGIC, ALU.mult,
                                        ALU.add).then_inc(ln2_start, 1)

            def choose(nt, logits):
                chain.link(nc.vector.max(top[nt][:], logits), const_done)
                nc.vector.max_index(top_at[nt][:], top[nt][:], logits).then_inc(job_free, 1)

            def choose_masks(nt, k):
                dve.wait_ge(job_free, k + 1)
                chain.link(nc.vector.tensor_tensor(chosen[nt][:], iota8[:].unsqueeze(1).to_broadcast([P, TOPK, E]),
                                                   top_at[nt][:, 0:TOPK].unsqueeze(2).to_broadcast([P, TOPK, E]),
                                                   ALU.is_equal))
                nc.vector.tensor_tensor(mask[nt][:], chosen[nt][:, 0, :], chosen[nt][:, 1, :], ALU.add).then_inc(mask_done, 1)

            def route(b, nt):
                m = b * 2 + nt
                chain.link(nc.vector.tensor_tensor(slot_m[nt][:], chosen[nt][:],
                                                   slot_e[nt][:].unsqueeze(1).to_broadcast([P, TOPK, E]), ALU.mult))
                dve.wait_ge(slots_free, m + 1)
                with nc.allow_low_precision(reason="slots are whole numbers below 2^24"):
                    nc.vector.tensor_reduce(slot[nt][:], slot_m[nt][:], AX.X, ALU.add)
                nc.vector.tensor_copy(entry[nt][:, :, 0], token[:, bass.ds(m, 1)].to_broadcast([P, TOPK]))
                dve.wait_ge(ratio_done, m + 1)
                chain.link(nc.vector.tensor_scalar(ratio[nt][:, 1:2], ratio[nt][:, 0:1], 1.0, None, ALU.add))
                chain.link(nc.vector.reciprocal(entry[nt][:, 0, 1:2], ratio[nt][:, 1:2]))
                nc.vector.tensor_tensor(entry[nt][:, 1, 1:2], entry[nt][:, 0, 1:2], ratio[nt][:, 0:1],
                                        ALU.mult).then_inc(route_done, 1)

            def stage_scale(n, power, bounds, up):
                dve.wait_ge(amc_reduced, n)
                chain.link(nc.vector.tensor_reduce(power, bounds, AX.X, ALU.max))
                chain.link(nc.vector.tensor_scalar(power.bitcast(U32), power.bitcast(U32), EXPONENT, None, ALU.bitwise_and),
                           const_done)
                nc.vector.tensor_scalar(up.bitcast(I32), power.bitcast(I32), -1.0, UP_W_OVER, ALU.mult,
                                        ALU.add).then_inc(upw_done, 1)

            def w2_max(experts, done):
                for e in experts:
                    dve.wait_ge(w2_in[e], 16)
                    for k in range(2):
                        ins = nc.vector.tensor_reduce(amc2[:, e, k:k + 1], w2_raw[e][:, 512 * k:512 * k + 512], AX.X, ALU.max,
                                                      apply_absolute_value=True)
                if done:
                    ins.then_inc(amc_maxed, 1)

            def w2_scale(late):
                g = slice(4 * late, 4 * late + 4)
                stage_scale(E + 1 + late, pw2[:, g], amc2_all[:, g], upw2[:, g])

            def w1_low(k):
                c = 512 * k
                dve.wait_ge(stage_high, 4 * (E - 1) + k + 1)
                nc.vector.scalar_tensor_tensor(out=w1_part(E - 1, 1, c), in0=stage[1][:, c:c + 512], scalar=upw[1][:],
                                               in1=w1_part(E - 1, 0, c), op0=ALU.mult, op1=ALU.subtract).then_inc(stage_low, 1)

            def split_low(e, chunks=range(4)):
                for k in chunks:
                    dve.wait_ge(stage_high, 4 * (E + e) + k + 1)
                    c = 512 * k
                    nc.vector.scalar_tensor_tensor(out=w2_part(e, 1, c), in0=w2_raw[e][:, c:c + 512], scalar=upw2[:, e:e + 1],
                                                   in1=w2_part(e, 0, c), op0=ALU.mult, op1=ALU.subtract).then_inc(stage_low, 1)

            def group_max(g, s, prev):
                dve.wait_ge(scores_full, g + 1)
                if prev or s >= 2:
                    dve.wait_ge(exp_done, g - 1)
                chain.link(nc.vector.tensor_reduce(nmax[s % 2][:], s_bank[s % 2][:, 0:GH * M].rearrange("p (h m) -> p h m", h=GH),
                                                   AX.X, ALU.max, negate=True))
                nc.vector.tensor_scalar(ebias[s % 2][:], nmax[s % 2][:], logit_scale[:], LN_UP_P, ALU.mult,
                                        ALU.add).then_inc(bias_done, 1)

            def pT_split(g, s):
                dve.wait_ge(pT_high, g + 1)
                low(pT[s % 2][:, 1], t_bank[0:M, :].rearrange("p (h n) -> p h n", h=GH), pT[s % 2][:, 0], 1.0, pT_low)

            def norm_o(g, s):
                bank = o_bank[s % 2][:, 0:GH * (DH + 1)].rearrange("p (h d) -> p h d", h=GH)
                dve.wait_ge(av_full, g + 1)
                chain.link(nc.vector.reciprocal(rsum[s % 2][:], bank[:, :, DH]))
                c = (s % 4) * GH * DH
                nc.vector.tensor_tensor(o[s % 8 // 4][:, c:c + GH * DH].rearrange("p (h d) -> p h d", h=GH), bank[:, :, 0:DH],
                                        rsum[s % 2][:].unsqueeze(2).to_broadcast([P, GH, DH]), ALU.mult).then_inc(norm_done, 1)

            for j in Jobs(PROLOGUE_JOBS, 0, 0).of(0):
                job(j, 0, 0, 0)

            LINKS = 36
            group_max(0, 0, False)

            def body(b, parity, prev, nxt):
                jobs = batch_jobs(b, prev, nxt)
                if prev:
                    chain.base, chain.n = (b - 1) * LINKS + after_first, 0
                for s in range(GROUPS):
                    for j in jobs.of(s, 0):
                        job(j, 1 - parity, b, b - 1, not prev)
                    if s < 7 or nxt:
                        group_max(b * 8 + s + 1, (s + 1) % 8, prev or s >= 1)
                    if prev or s >= 1:
                        pT_split(b * 8 + s - 1, s - 1)
                    for j in jobs.of(s, 1):
                        job(j, 1 - parity, b, b - 1, not prev)
                    if prev or s >= 2:
                        norm_o(b * 8 + s - 2, s - 2)
                    if prev and s == ROUTE_STEPS[1]:
                        route(b - 1, 1)
                    if s == 7:
                        stage_scale(b + 1, pw1[:, bass.ds(b, 1)], amc_all[parity][:], upw[parity][:])
                    for j in jobs.of(s, 2):
                        job(j, 1 - parity, b, b - 1, not prev)
                    if prev and s == ROUTE_STEPS[0]:
                        route(b - 1, 0)
                assert not prev or not nxt or chain.n == LINKS, chain.n

            body(0, 0, False, True)
            after_first = chain.base + chain.n
            with dve.Fori(0, (B - 2) // 2) as i:
                body(i * 2 + 1, 1, True, True)
                body(i * 2 + 2, 0, True, True)
            body(B - 1, (B - 1) % 2, True, False)
            jobs = epilogue_jobs()
            pT_split(8 * B - 1, 7)
            norm_o(8 * B - 2, 6)
            for s in range(8, 14):
                if s == 9:
                    norm_o(8 * B - 1, 7)
                for j in jobs.of(s):
                    job(j, 0, B, B - 1)
                if s == 9:
                    dve.wait_ge(stage_low, 4 * (E - 1))
                    w1_low(0)
                    w2_max(W2_EARLY, True)
                if s == 10:
                    w1_low(1)
                if s == 11:
                    w1_low(2)
                    w1_low(3)
                    w2_scale(False)
                if s in (11, 13):
                    route(B - 1, int(s == 13))

            count, tiles, upto, frm, cmp_p, e_p, f_p, y8 = (small8[:, k, :] for k in range(8))
            h8 = tmp[:, 0:E]
            chain.link(nc.vector.tensor_tensor(count, base[0][:], seg[:], ALU.subtract))
            chain.link(nc.vector.tensor_scalar(small8i[:, 0, :], count, float(P - 1), None, ALU.add))
            chain.link(nc.vector.tensor_scalar(small8i[:, 1, :], small8i[:, 0, :], 7, None, ALU.arith_shift_right))
            chain.link(nc.vector.tensor_copy(tiles, small8i[:, 1, :]))
            chain.link(nc.vector.memset(count, 1.0))
            chain.link(nc.vector.tensor_tensor_scan(upto, count, tiles, 0.0, ALU.mult, ALU.add))
            chain.link(nc.vector.tensor_tensor(frm, upto, tiles, ALU.subtract))
            chain.link(nc.vector.tensor_scalar(cmp_p, upto, row_id[:], None, ALU.is_le))
            chain.link(nc.vector.tensor_reduce(e_p[:, 0:1], cmp_p, AX.X, ALU.add))
            chain.link(nc.vector.tensor_scalar(f_p, iota8[:], e_p[:, 0:1], None, ALU.is_equal))
            chain.link(nc.vector.tensor_tensor(cmp_p, f_p, frm, ALU.mult))
            chain.link(nc.vector.tensor_reduce(e_p[:, 1:2], cmp_p, AX.X, ALU.add))
            chain.link(nc.vector.tensor_tensor(e_p[:, 2:3], row_id[:], e_p[:, 1:2], ALU.subtract))
            chain.link(nc.vector.scalar_tensor_tensor(out=e_p[:, 3:4], in0=e_p[:, 0:1], scalar=float(BLOCKS), in1=e_p[:, 2:3],
                                                      op0=ALU.mult, op1=ALU.add))
            nc.vector.tensor_scalar(blk[:], e_p[:, 3:4], float(E * BLOCKS), None, ALU.min).then_inc(blk_done, 1)
            chain.link(nc.vector.tensor_tensor(by_expert[:], upto.unsqueeze(1).to_broadcast([P, TILES, E]),
                                               tile_id[:, 0:TILES].unsqueeze(2).to_broadcast([P, TILES, E]), ALU.is_le))
            chain.link(nc.vector.tensor_reduce(expert_f[:], by_expert[:], AX.X, ALU.add))
            chain.link(nc.vector.tensor_scalar(expert_f[:], expert_f[:], float(E - 1), None, ALU.min))
            nc.vector.tensor_copy(expert_of[:], expert_f[:])
            chain.link(nc.vector.tensor_tensor(one_hot[:], iota8[:].unsqueeze(1).to_broadcast([P, TILES, E]),
                                               expert_f[:].unsqueeze(2).to_broadcast([P, TILES, E]), ALU.is_equal))

            for e in W2_EARLY:
                split_low(e)
            dve.wait_ge(found_T, 1)
            nc.vector.tensor_copy(row_of[:], j_bank[0][:, 0:TILES]).then_inc(rows_done, 1)
            chain.link(nc.vector.tensor_copy(gate_y[:], j_bank[0][:, 64:64 + TILES]))
            chain.link(nc.vector.reciprocal(h8, pw1[:]))
            chain.link(nc.vector.tensor_scalar(h8, h8, UP_H, None, ALU.mult))
            chain.link(nc.vector.tensor_scalar(count, pw1[:], 1.0 / (UP_W * UP_X), None, ALU.mult))

            def by_tile(vec, dst):
                chain.link(nc.vector.tensor_tensor(by_expert[:], one_hot[:], vec.unsqueeze(1).to_broadcast([P, TILES, E]),
                                                   ALU.mult))
                chain.link(nc.vector.tensor_reduce(dst[:], by_expert[:], AX.X, ALU.add))

            by_tile(count, z_scale)
            by_tile(h8, h_scale)
            nc.vector.tensor_copy(tmp[:, 0:1], z_scale[:, 0:1]).then_inc(tables_done, 1)
            w2_scale(True)
            split_low(4, range(POOL_LOW.get(4, 4)))

            def y_scales():
                chain.link(nc.vector.scalar_tensor_tensor(out=y8, in0=pw1[:], scalar=2.0 ** -20, in1=pw2[:], op0=ALU.mult,
                                                          op1=ALU.mult))
                chain.link(nc.vector.tensor_scalar(y8, y8, tg[:, 1:2], None, ALU.mult))
                by_tile(y8, y_scale)
                chain.link(nc.vector.tensor_tensor(gate_y[:], gate_y[:], y_scale[:], ALU.mult))

            def x_low(t, par):
                dve.wait_ge(xs_high, t + 1)
                nc.vector.tensor_tensor(xsT[par][:, 1].rearrange("p k n -> p (k n)"), s_bank[par][:, 0:D],
                                        xsT[par][:, 0].rearrange("p k n -> p (k n)"), ALU.subtract).then_inc(xs_low, 1)

            def h_split(t, par):
                for a in range(2):
                    dve.wait_ge(h_high, t * 2 + a + 1)
                    nc.vector.scalar_tensor_tensor(out=hT[par][:, 1, 4 * a:4 * a + 4, :],
                                                   in0=hT_bank[a][:].rearrange("p (c n) -> p c n", c=4),
                                                   scalar=h_scale[:, bass.ds(t, 1)], in1=hT[par][:, 0, 4 * a:4 * a + 4, :],
                                                   op0=ALU.mult, op1=ALU.subtract).then_inc(h_low, 1)

            def y_gated(t, par, first):
                dve.wait_ge(y_full, t + 1)
                if not first:
                    dve.wait_ge(y_added, t * 16 - 16)
                nc.vector.tensor_scalar(yt[par][:], j_bank[par][:, 0:D], gate_y[:, bass.ds(t, 1)], None,
                                        ALU.mult).then_inc(y_done, 1)

            x_low(0, 0)

            def step(t, par, buf, before, first, last):
                if first:
                    split_low(5, range(POOL_LOW.get(5, 4)))
                if not last:
                    x_low(t + 1, 1 - par)
                if first:
                    y_scales()
                    split_low(6, range(POOL_LOW.get(6, 4)))
                else:
                    y_gated(t - 1, 1 - par, isinstance(t, int) and t < 3)
                h_split(t, par)
                if first:
                    split_low(7, range(POOL_LOW.get(7, 4)))

            run_tiles(dve, step)
            y_gated(TILES - 1, (TILES - 1) % 2, False)

        @block.tensor
        def _(pe):
            pe.wait_ge(const_done, 9)

            def three(out, lhs, rhs):
                n = len(lhs)
                for i in range(n):
                    for a, c in ((0, 0), (0, 1), (1, 0)):
                        ins = pe.matmul(out, lhs[i](a), rhs[i](c), start=(i == 0 and a + c == 0),
                                        stop=(i == n - 1 and a == 1))
                return ins

            def job(j, par, b, jobs):
                name, k, bank, h = j
                dst = j_bank[bank]
                if not (isinstance(k, int) and k < JOB_BANKS):
                    pe.wait_ge(job_free, k - JOB_BANKS + 1)
                if name == "XT":
                    pe.wait_ge(xn_done, b + 1)
                    for kc in range(KC):
                        for t in range(NT):
                            ins = pe.transpose(dst[:, (kc * NT + t) * P:(kc * NT + t + 1) * P],
                                               xn[:, t, kc * P:(kc + 1) * P], ident[:])
                elif name[0] == "K":
                    c = 4 * (name == "Kb")
                    for q in range(4):
                        ins = three(dst[:, q * M:(q + 1) * M],
                                    [lambda a, kc=kc, q=q: wkvs[:, a, kc, (c + q) * P:(c + q + 1) * P] for kc in range(KC)],
                                    [lambda a, kc=kc: ctxs[:, a, kc, bass.ds(b * M, M)] for kc in range(KC)])
                elif name[0] == "V":
                    c = INNER + 512 * (name == "Vb")
                    ins = three(dst[0:M, :],
                                [lambda a, kc=kc: ctxs[:, a, kc, bass.ds(b * M, M)] for kc in range(KC)],
                                [lambda a, kc=kc: wkvs[:, a, kc, c:c + 512] for kc in range(KC)])
                elif name[0] == "Q":
                    if name == "Q0":
                        pe.wait_ge(job_free, jobs.at["XT"][1] + 1)
                    c = 2 * int(name[1])
                    for q in range(2):
                        ins = three(dst[:, q * N:(q + 1) * N],
                                    [lambda a, kc=kc, q=q: wqs[:, a, kc, (c + q) * P:(c + q + 1) * P] for kc in range(KC)],
                                    [lambda a, kc=kc: xnT[:, a, kc, :] for kc in range(KC)])
                elif name[:2] == "OT":
                    nt, half = int(name[2]), name[3] == "b"
                    pe.wait_ge(norm_done, (b * 2 + nt) * 4 + 4)
                    for q in range(4):
                        c = (4 * half + q) * P
                        ins = pe.transpose(dst[:, q * P:(q + 1) * P], o[nt][:, c:c + P], ident[:])
                elif name[:2] == "PJ":
                    pe.wait_ge(job_free, jobs.at["OT" + name[2] + "b"][1] + 1)
                    ins = three(dst[:, 0:D], [lambda a, ic=ic: oT[:, a, ic, :] for ic in range(IC)],
                                [lambda a, ic=ic: wos[:, a, ic, :] for ic in range(IC)])
                elif name[:3] == "X2T":
                    nt = int(name[3])
                    pe.wait_ge(xn2_done, b * 2 + nt + 1)
                    for kc in range(KC):
                        ins = pe.transpose(dst[:, kc * P:(kc + 1) * P], xn2[nt][:, kc * P:(kc + 1) * P], ident[:])
                elif name[:2] == "LG":
                    pe.wait_ge(router_scaled, 1)
                    nt = int(name[2])
                    pe.wait_ge(job_free, jobs.at["X2T" + name[2]][1] + 1)
                    for kc in range(KC):
                        ins = pe.matmul(dst[:, 0:E], xn2T[nt][:, kc, :], wrs[:, kc, :], start=(kc == 0), stop=(kc == KC - 1))
                else:
                    nt = int(name[2])
                    pe.wait_ge(mask_done, b * 2 + nt + 1)
                    pe.matmul(dst[:, 0:E], upper[:], mask[nt][:], start=True, stop=True)
                    ins = pe.matmul(dst[:, E:2 * E], ones[:], mask[nt][:], start=True, stop=True)
                ins.then_inc(job_full, 1)

            def scores(g, s, par, prev):
                if prev or s >= 2:
                    pe.wait_ge(exp_done, g - 1)
                for q in range(2):
                    pair, t = 2 * (s % 4) + q, s // 4
                    ins = three(s_bank[s % 2][:, q * 2 * M:(q + 1) * 2 * M],
                                [lambda a: qT[par][:, a, pair, t * P:(t + 1) * P]], [lambda a: kT[par][:, a, pair, :]])
                ins.then_inc(scores_full, 1)

            def transposes(g, s, first):
                pe.wait_ge(exp_done, g + 1)
                if not first:
                    pe.wait_ge(pT_low, g)
                for h in range(GH):
                    ins = pe.transpose(t_bank[0:M, h * P:(h + 1) * P], pr[s % 2][:, h, :], ident[:])
                ins.then_inc(pT_full, 1)

            def values(g, s, par, first):
                pe.wait_ge(pT_low, g + 1)
                if not first:
                    pe.wait_ge(norm_done, g - 1)
                for h in range(GH):
                    head = (s % 4) * GH + h
                    ins = three(o_bank[s % 2][:, h * (DH + 1):(h + 1) * (DH + 1)],
                                [lambda a: pT[s % 2][:, a, h, :]], [lambda a: v[par][:, a, head, :]])
                ins.then_inc(av_full, 1)

            pe.wait_ge(w_low, KC * 3 + IC)
            pe.wait_ge(zero_done, 4)
            pro = Jobs(PROLOGUE_JOBS, 0, 0)
            for j in pro.of(0):
                job(j, 0, 0, pro)

            pe.wait_ge(job_free, len(PROLOGUE_JOBS))
            scores(0, 0, 0, False)
            KIND = {name: kind for _, _, name, kind in JOBS}
            AFTER_Q3 = len(JOBS) - 1 - [name for _, _, name, _ in JOBS].index("Q3")

            def body(b, parity, prev, nxt):
                jobs = batch_jobs(b, prev, nxt)

                def run(js):
                    for j in js:
                        kind = KIND[j[0]]
                        job(j, 1 - parity, b + 1 if kind == "n" else b - 1 if kind == "p" else b, jobs)

                for s in range(GROUPS):
                    if s < 7:
                        if s == 0 and prev:
                            pe.wait_ge(job_free, jobs.k0 - AFTER_Q3)
                        scores(b * 8 + s + 1, s + 1, parity, prev or s >= 1)
                    elif nxt:
                        pe.wait_ge(job_free, jobs.at["Q0"][1] + 1)
                        scores(b * 8 + 8, 0, 1 - parity, True)
                    run(jobs.of(s, 0))
                    if prev or s >= 1:
                        transposes(b * 8 + s - 1, (s - 1) % 8, not prev and s < 2)
                    run(jobs.of(s, 1))
                    if prev or s >= 2:
                        values(b * 8 + s - 2, (s - 2) % 8, parity if s >= 2 else 1 - parity, not prev and s < 4)
                    run(jobs.of(s, 2))

            run_batches(pe, body)
            jobs = epilogue_jobs()
            transposes(8 * B - 1, 7, False)
            values(8 * B - 2, 6, (B - 1) % 2, False)
            for s in range(8, 14):
                if s == 9:
                    values(8 * B - 1, 7, (B - 1) % 2, False)
                for j in jobs.of(s):
                    job(j, 0, B - 1, jobs)

            pe.wait_ge(found_in, 16)
            pe.wait_ge(job_free, jobs.k_end)
            f = found[0:TILES, :].rearrange("t (r c) -> t r c", c=2)
            pe.transpose(j_bank[0][:, 0:TILES], f[:, :, 0], ident[0:TILES, 0:TILES])
            pe.transpose(j_bank[0][:, 64:64 + TILES], f[:, :, 1], ident[0:TILES, 0:TILES]).then_inc(found_T, 1)

            def tile_T(t, par, buf, before, first):
                pe.wait_ge(xg_in[buf], before * 16 + 16)
                if not first:
                    pe.wait_ge(xs_low, t - 1)
                for kc in range(KC):
                    ins = pe.transpose(s_bank[par][:, kc * P:(kc + 1) * P], xg[buf][:, kc * P:(kc + 1) * P], ident[:])
                ins.then_inc(xs_full, 1)

            def expert(t):
                return pe.value_load(expert_of[0:1, bass.ds(t, 1)], min_val=0, max_val=E - 1)

            def up_product(e, t, par, first):
                pe.wait_ge(xs_low, t + 1)
                if not first:
                    pe.wait_ge(silu_done, t * 2)
                for a in range(2):
                    three(z_bank[a][:], [lambda p, kc=kc: xsT[par][:, p, kc, :] for kc in range(KC)],
                          [lambda p, kc=kc: w1s[:, bass.ds(e, 1), p, kc, 512 * a:512 * a + 512].rearrange("p e f -> p (e f)")
                           for kc in range(KC)]).then_inc(z_full, 1)

            def hidden_T(t, par, first):
                if not first:
                    pe.wait_ge(h_low, t * 2)
                for a in range(2):
                    pe.wait_ge(silu_done, t * 2 + a + 1)
                    for c in range(4):
                        ins = pe.transpose(hT_bank[a][:, c * P:(c + 1) * P], hf[par][:, (4 * a + c) * P:(4 * a + c + 1) * P],
                                           ident[:])
                    ins.then_inc(hT_full, 1)

            def down_product(e, t, par, first):
                pe.wait_ge(h_low, t * 2 + 2)
                if not first:
                    pe.wait_ge(y_done, t - 1)
                ins = three(j_bank[par][:, 0:D], [lambda a, fc=fc: hT[par][:, a, fc, :] for fc in range(FC)],
                            [lambda a, fc=fc: w2s[:, bass.ds(e, 1), a, fc, :].rearrange("p e d -> p (e d)") for fc in range(FC)])
                ins.then_inc(y_full, 1)

            pe.wait_ge(tables_done, 1)
            pe.wait_ge(stage_low, 4 * E)
            tile_T(0, 0, 0, 0, True)

            last_expert = [None]

            def step(t, par, buf, before, first, last):
                reload = last or (not isinstance(t, int) and buf == (2 + 1) % XG)
                e_before = expert(t - 1) if reload else last_expert[0]
                e = last_expert[0] = expert(t)
                if not last:
                    tile_T(t + 1, 1 - par, buf, before, first)
                up_product(e, t, par, first)
                if isinstance(t, int) and t == 1:
                    pe.wait_ge(stage_low, 8 * E - sum(4 - k for k in POOL_LOW.values()))
                    pe.wait_ge(w2_low_pool, sum(4 - k for k in POOL_LOW.values()))
                if not first:
                    down_product(e_before, t - 1, 1 - par, isinstance(t, int) and t < 3)
                hidden_T(t, par, first)

            run_tiles(pe, step)
            down_product(last_expert[0], TILES - 1, (TILES - 1) % 2, False)


INPUTS = ("x", "ctxT", "wq", "wkv", "wo", "bo", "gx", "gf", "w1", "w2", "wr")


def kernel(x, ctx_1024, g_xattn, g_ffn, L0_xattn_w_q, L0_xattn_w_kv, L0_xattn_w_out, L0_xattn_b_out, L0_ffn_W1, L0_ffn_W2,
           L0_ffn_Wr):
    import concourse.bacc as bacc
    from concourse.bass_utils import run_bass_kernel_spmd

    def rows(a, k):
        return np.asarray(a).reshape(k, P, -1).transpose(1, 0, 2)

    layout = {
        "x": np.asarray(x).reshape(T, D),
        "ctxT": np.asarray(ctx_1024).reshape(B * M, KC, P).transpose(2, 1, 0),
        "wq": rows(L0_xattn_w_q, KC),
        "wkv": rows(L0_xattn_w_kv, KC),
        "wo": rows(L0_xattn_w_out, IC),
        "bo": np.asarray(L0_xattn_b_out),
        "gx": np.asarray(g_xattn),
        "gf": np.asarray(g_ffn),
        "w1": np.asarray(L0_ffn_W1).reshape(E, DFF, KC, P).transpose(0, 3, 2, 1),
        "w2": np.asarray(L0_ffn_W2).reshape(E, D, FC, P).transpose(0, 3, 2, 1),
        "wr": np.asarray(L0_ffn_Wr).reshape(E, KC, P).transpose(2, 1, 0),
    }
    nc = bacc.Bacc("TRN2", target_bir_lowering=False, num_devices=1)
    arrays = {f"in_{name}": np.ascontiguousarray(layout[name]) for name in INPUTS}
    args = [nc.dram_tensor(f"in_{name}", arrays[f"in_{name}"].shape, F32, kind="ExternalInput").ap() for name in INPUTS]
    out = nc.dram_tensor("out", (T + P, D), F32, kind="ExternalOutput").ap()
    xn2_dram = nc.dram_tensor("xn2", (T + P, D), F32, kind="Internal").ap()
    table = nc.dram_tensor("table", (P * (P + 1), 2), F32, kind="Internal").ap()
    build(nc, *args, out, xn2_dram, table)
    result = run_bass_kernel_spmd(nc, [arrays], core_ids=[0])
    return result.results[0]["out"][:T].reshape(B, N, D)
```
